# Optimizing a Trainium2 kernel written in Bass

```python
import numpy as np
import jax
import jax.numpy as jnp

def _softmax(x, axis=-1):
    return jax.nn.softmax(x, axis=axis)

def _gelu(x):
    return jax.nn.gelu(x, approximate=True)

def _silu(x):
    return jax.nn.silu(x)

def _sigmoid(x):
    return jax.nn.sigmoid(x)

def _layernorm(x, axis=-1, eps=1e-05):
    m = jnp.mean(x, axis=axis, keepdims=True)
    v = jnp.var(x, axis=axis, keepdims=True)
    return (x - m) / jnp.sqrt(v + eps)

def _scatter_add(tgt, idx, src, axis=0):
    return tgt.at[idx].add(src)

def _segment_sum(src, seg, n):
    return jax.ops.segment_sum(src, seg, n)
kernel_name = 'mk_xattn_ffn_d1_seqx_r4_776521'

def setup_inputs(seed: int=0):
    np.random.seed(seed)
    _w = jnp.asarray

    def _rec_inputs():
        import jax
        import jax.numpy as jnp
        _rk = jax.random.key(seed)
        x = 0.0002417 + 0.9998 * jax.random.normal(jax.random.fold_in(_rk, 1), (32, 256, 256), jnp.float32)
        _lenS = 256 - jax.random.randint(jax.random.fold_in(_rk, 7), (32,), 0, max(1, 256 // 4) + 1, jnp.int32)
        _lenS2 = 77 - jax.random.randint(jax.random.fold_in(_rk, 8), (32,), 0, max(1, 77 // 4) + 1, jnp.int32)
        _ctx_1024P = jax.random.normal(jax.random.fold_in(_rk, 11), (32, 16, 256), jnp.float32)
        _ctx_1024c = jax.random.dirichlet(jax.random.fold_in(_rk, 511), 0.3 * jnp.ones((16,), jnp.float32), (32, 77))
        _ctx_1024t = jnp.einsum('bsk,bkd->bsd', _ctx_1024c, _ctx_1024P)
        _ctx_1024t = _ctx_1024t * jax.lax.rsqrt(jnp.mean(jnp.square(_ctx_1024t)) + 1e-12) * 0.953939
        ctx_1024 = 7.22013e-05 + 1.00017 * (_ctx_1024t + 0.3 * jax.random.normal(jax.random.fold_in(_rk, 611), (32, 77, 256), jnp.float32))
        return (x, ctx_1024)
    x, ctx_1024 = _rec_inputs()

    def _L0_xattn_setup():
        import jax, jax.numpy as jnp
        import numpy as np
        D_MODEL = 256
        B, S = (4, 512)
        key = jax.random.key(seed)
        ks = jax.random.split(key, 10)
        s = 1.0 / np.sqrt(D_MODEL)
        return {'k': jax.random.normal(ks[0], (B, S, D_MODEL), jnp.float32), 'v': jax.random.normal(ks[1], (B, S, D_MODEL), jnp.float32), 'q': jax.random.normal(ks[2], (B, S, D_MODEL), jnp.float32), 'Wk': jax.random.normal(ks[3], (D_MODEL, D_MODEL), jnp.float32) * s, 'Wv': jax.random.normal(ks[4], (D_MODEL, D_MODEL), jnp.float32) * s, 'bv': jnp.zeros((D_MODEL,), jnp.float32), 'Wq': jax.random.normal(ks[5], (D_MODEL, D_MODEL), jnp.float32) * s, 'bq': jnp.zeros((D_MODEL,), jnp.float32), 'Wo': jax.random.normal(ks[6], (D_MODEL, D_MODEL), jnp.float32) * s, 'bo': jnp.zeros((D_MODEL,), jnp.float32)}
    _L0_xattn_all = _L0_xattn_setup()
    _L0_xattn_in = {k: v for k, v in _L0_xattn_all.items() if k in ('Wk', 'Wv', 'bv', 'Wq', 'bq', 'Wo', 'bo')}
    del _L0_xattn_all

    def _L0_ffn_setup():
        import jax, jax.numpy as jnp
        import numpy as np
        B, S = (2, 256)
        E, TOPK = (8, 2)
        HIDDEN, HEADS, NSLOTS = (256, 4, 64)
        HEAD_K = HIDDEN // HEADS
        HEAD_V = HIDDEN // HEADS
        GATE_NORM = 8.0
        SCALE = 1.0
        EPS = 1e-05
        CHUNK = 64
        CAP = S

        def rms_norm(x, w, eps=EPS):
            y = x * jax.lax.rsqrt(jnp.mean(x * x, axis=-1, keepdims=True) + eps)
            return y * w

        def swish(x):
            return x * jax.nn.sigmoid(x)

        def gsa_chunk(q, k, v, s, g):
            EBH = q.shape[:3]
            T, Dk, Dv, M = (q.shape[3], q.shape[-1], v.shape[-1], s.shape[-1])
            Nc = T // CHUNK

            def to_chunks(x):
                return jnp.moveaxis(x.reshape(EBH + (Nc, CHUNK, x.shape[-1])), 3, 0)
            qc, kc, vc, sc, gc = map(to_chunks, (q, k, v, s, g))
            Gc = jnp.cumsum(gc, axis=-2)
            tril = jnp.tril(jnp.ones((CHUNK, CHUNK), q.dtype))
            hk0 = jnp.zeros(EBH + (Dk, M), q.dtype)
            hv0 = jnp.zeros(EBH + (M, Dv), q.dtype)

            def step(carry, xs):
                hk, hv = carry
                qt, kt, vt, st, Gt = xs
                dec = jnp.exp(Gt)
                s_in = st * jnp.exp(-Gt)
                A = jnp.einsum('ebhik,ebhjk->ebhij', qt, kt) * SCALE * tril
                ok = dec * (jnp.einsum('ebhij,ebhjm->ebhim', A, s_in) + SCALE * jnp.einsum('ebhik,ebhkm->ebhim', qt, hk))
                qv = jax.nn.softmax(ok, axis=-1)
                qvg = qv * dec
                Tm = jnp.einsum('ebhim,ebhjm->ebhij', qvg, s_in) * tril
                ov = jnp.einsum('ebhij,ebhjd->ebhid', Tm, vt) + jnp.einsum('ebhim,ebhmd->ebhid', qvg, hv)
                gl = jnp.exp(Gt[..., -1, :])
                s_rem = st * jnp.exp(Gt[..., -1:, :] - Gt)
                hk = hk * gl[..., None, :] + jnp.einsum('ebhck,ebhcm->ebhkm', kt, s_rem)
                hv = hv * gl[..., :, None] + jnp.einsum('ebhcm,ebhcd->ebhmd', s_rem, vt)
                return ((hk, hv), ov)
            _, ov = jax.lax.scan(step, (hk0, hv0), (qc, kc, vc, sc, Gc))
            return jnp.moveaxis(ov, 0, 3).reshape(EBH + (T, Dv))

        def forward(hidden_states, norm_w, Wg, Wq, Wk, Wv, Wf, gnorm_w, Wo):
            b, s, d = hidden_states.shape
            x = rms_norm(hidden_states, norm_w)
            scores = jax.nn.softmax(jnp.einsum('bsd,ed->bse', x, Wg), axis=-1)
            rw, sel = jax.lax.top_k(scores, TOPK)
            rw = rw / jnp.sum(rw, axis=-1, keepdims=True)
            routing_mask = jax.nn.one_hot(sel, E, dtype=jnp.int32).sum(2)
            s_eff = s * TOPK
            xr = jnp.repeat(x, TOPK, axis=1).reshape(b * s_eff, d)
            batch_idx = jnp.repeat(jnp.arange(b), s_eff)
            combined = batch_idx * E + sel.reshape(-1)
            sorted_indices = jnp.argsort(combined)
            x_sorted = xr[sorted_indices]
            counts = routing_mask.sum(1)
            flat_end = (jnp.cumsum(counts, axis=1) + jnp.arange(b)[:, None] * s_eff).reshape(-1)
            start = jnp.concatenate([jnp.zeros((1,), flat_end.dtype), flat_end[:-1]])
            pos = jnp.arange(CAP)[None, :] + start[:, None]
            trunc = pos + counts.reshape(-1)[:, None] - CAP
            mask = (trunc < flat_end[:, None]) & (trunc >= 0) & (trunc >= start[:, None])
            trunc = jnp.where(mask, trunc, 0)
            xe = x_sorted[trunc.reshape(-1)].reshape(b * E, CAP, d) * mask[..., None]
            xe = xe.reshape(b, E, CAP, d).transpose(1, 0, 2, 3)
            q = jnp.einsum('ebtd,kd->ebtk', xe, Wq).reshape(E, b, CAP, HEADS, HEAD_K)
            k = jnp.einsum('ebtd,ekd->ebtk', xe, Wk).reshape(E, b, CAP, HEADS, HEAD_K)
            v = jnp.einsum('ebtd,ekd->ebtk', xe, Wv).reshape(E, b, CAP, HEADS, HEAD_V)
            f = jnp.einsum('ebtd,ekd->ebtk', xe, Wf).reshape(E, b, CAP, HEADS, NSLOTS)
            g = jax.nn.log_sigmoid(f) / GATE_NORM
            slot = 1.0 - jnp.exp(g)
            q, k = (swish(q), swish(k))
            tr = lambda a: a.transpose(0, 1, 3, 2, 4)
            o = gsa_chunk(tr(q), tr(k), tr(v), tr(slot), tr(g)).transpose(0, 1, 3, 2, 4)
            gathered = o.transpose(1, 0, 2, 3, 4).reshape(b * E * CAP, HEADS, HEAD_V)
            gathered = gathered * mask.reshape(-1)[:, None, None]
            resort = jnp.zeros((b * s_eff, HEADS, HEAD_V), gathered.dtype).at[trunc.reshape(-1)].add(gathered)
            restored = resort[jnp.argsort(sorted_indices)].reshape(b, s, TOPK, HEADS, HEAD_V)
            out = (restored * rw[..., None, None]).sum(2).reshape(b, s, HIDDEN)
            return jnp.einsum('bsd,od->bso', rms_norm(out, gnorm_w), Wo)
        key = jax.random.key(seed)
        ks = jax.random.split(key, 8)
        w = 0.02
        return {'hidden_states': jax.random.normal(ks[0], (B, S, HIDDEN), jnp.float32), 'norm_w': jnp.ones((HIDDEN,), jnp.float32), 'Wg': jax.random.normal(ks[1], (E, HIDDEN), jnp.float32) * w, 'Wq': jax.random.normal(ks[2], (HIDDEN, HIDDEN), jnp.float32) * w, 'Wk': jax.random.normal(ks[3], (E, HIDDEN, HIDDEN), jnp.float32) * w, 'Wv': jax.random.normal(ks[4], (E, HIDDEN, HIDDEN), jnp.float32) * w, 'Wf': jax.random.normal(ks[5], (E, HEADS * NSLOTS, HIDDEN), jnp.float32) * w, 'gnorm_w': jnp.ones((HIDDEN,), jnp.float32), 'Wo': jax.random.normal(ks[6], (HIDDEN, HIDDEN), jnp.float32) * w}
    _L0_ffn_all = _L0_ffn_setup()
    _L0_ffn_in = {k: v for k, v in _L0_ffn_all.items() if k in ('norm_w', 'Wg', 'Wq', 'Wk', 'Wv', 'Wf', 'gnorm_w', 'Wo')}
    del _L0_ffn_all
    return {'x': x, 'ctx_1024': ctx_1024, 'L0_xattn_Wk': _L0_xattn_in['Wk'], 'L0_xattn_Wv': _L0_xattn_in['Wv'], 'L0_xattn_bv': _L0_xattn_in['bv'], 'L0_xattn_Wq': _L0_xattn_in['Wq'], 'L0_xattn_bq': _L0_xattn_in['bq'], 'L0_xattn_Wo': _L0_xattn_in['Wo'], 'L0_xattn_bo': _L0_xattn_in['bo'], 'L0_ffn_norm_w': _L0_ffn_in['norm_w'], 'L0_ffn_Wg': _L0_ffn_in['Wg'], 'L0_ffn_Wq': _L0_ffn_in['Wq'], 'L0_ffn_Wk': _L0_ffn_in['Wk'], 'L0_ffn_Wv': _L0_ffn_in['Wv'], 'L0_ffn_Wf': _L0_ffn_in['Wf'], 'L0_ffn_gnorm_w': _L0_ffn_in['gnorm_w'], 'L0_ffn_Wo': _L0_ffn_in['Wo']}

def reference(x, ctx_1024, L0_xattn_Wk, L0_xattn_Wv, L0_xattn_bv, L0_xattn_Wq, L0_xattn_bq, L0_xattn_Wo, L0_xattn_bo, L0_ffn_norm_w, L0_ffn_Wg, L0_ffn_Wq, L0_ffn_Wk, L0_ffn_Wv, L0_ffn_Wf, L0_ffn_gnorm_w, L0_ffn_Wo):
    import jax
    import jax.numpy as jnp

    def _L0_xattn_ref(k, v, q, Wk, Wv, bv, Wq, bq, Wo, bo):
        import jax, jax.numpy as jnp
        import numpy as np
        D_MODEL = 256
        B, S = (4, 512)
        kp = jnp.einsum('bsd,ed->bse', k, Wk)
        vp = jnp.einsum('bsd,ed->bse', v, Wv) + bv
        qp = jnp.einsum('bsd,ed->bse', q, Wq) + bq
        scale = 1.0 / jnp.sqrt(jnp.float32(kp.shape[-1]))
        scores = jnp.einsum('bqd,bkd->bqk', qp, kp) * scale
        probs = jax.nn.softmax(scores, axis=-1)
        ctx = jnp.einsum('bqk,bkd->bqd', probs, vp)
        return jnp.einsum('bqd,ed->bqe', ctx, Wo) + bo

    def _L0_ffn_ref(hidden_states, norm_w, Wg, Wq, Wk, Wv, Wf, gnorm_w, Wo):
        import jax, jax.numpy as jnp
        import numpy as np
        B, S = (2, 256)
        E, TOPK = (8, 2)
        HIDDEN, HEADS, NSLOTS = (256, 4, 64)
        HEAD_K = HIDDEN // HEADS
        HEAD_V = HIDDEN // HEADS
        GATE_NORM = 8.0
        SCALE = 1.0
        EPS = 1e-05
        CHUNK = 64
        CAP = S

        def rms_norm(x, w, eps=EPS):
            y = x * jax.lax.rsqrt(jnp.mean(x * x, axis=-1, keepdims=True) + eps)
            return y * w

        def swish(x):
            return x * jax.nn.sigmoid(x)

        def gsa_chunk(q, k, v, s, g):
            EBH = q.shape[:3]
            T, Dk, Dv, M = (q.shape[3], q.shape[-1], v.shape[-1], s.shape[-1])
            Nc = T // CHUNK

            def to_chunks(x):
                return jnp.moveaxis(x.reshape(EBH + (Nc, CHUNK, x.shape[-1])), 3, 0)
            qc, kc, vc, sc, gc = map(to_chunks, (q, k, v, s, g))
            Gc = jnp.cumsum(gc, axis=-2)
            tril = jnp.tril(jnp.ones((CHUNK, CHUNK), q.dtype))
            hk0 = jnp.zeros(EBH + (Dk, M), q.dtype)
            hv0 = jnp.zeros(EBH + (M, Dv), q.dtype)

            def step(carry, xs):
                hk, hv = carry
                qt, kt, vt, st, Gt = xs
                dec = jnp.exp(Gt)
                s_in = st * jnp.exp(-Gt)
                A = jnp.einsum('ebhik,ebhjk->ebhij', qt, kt) * SCALE * tril
                ok = dec * (jnp.einsum('ebhij,ebhjm->ebhim', A, s_in) + SCALE * jnp.einsum('ebhik,ebhkm->ebhim', qt, hk))
                qv = jax.nn.softmax(ok, axis=-1)
                qvg = qv * dec
                Tm = jnp.einsum('ebhim,ebhjm->ebhij', qvg, s_in) * tril
                ov = jnp.einsum('ebhij,ebhjd->ebhid', Tm, vt) + jnp.einsum('ebhim,ebhmd->ebhid', qvg, hv)
                gl = jnp.exp(Gt[..., -1, :])
                s_rem = st * jnp.exp(Gt[..., -1:, :] - Gt)
                hk = hk * gl[..., None, :] + jnp.einsum('ebhck,ebhcm->ebhkm', kt, s_rem)
                hv = hv * gl[..., :, None] + jnp.einsum('ebhcm,ebhcd->ebhmd', s_rem, vt)
                return ((hk, hv), ov)
            _, ov = jax.lax.scan(step, (hk0, hv0), (qc, kc, vc, sc, Gc))
            return jnp.moveaxis(ov, 0, 3).reshape(EBH + (T, Dv))

        def forward(hidden_states, norm_w, Wg, Wq, Wk, Wv, Wf, gnorm_w, Wo):
            b, s, d = hidden_states.shape
            x = rms_norm(hidden_states, norm_w)
            scores = jax.nn.softmax(jnp.einsum('bsd,ed->bse', x, Wg), axis=-1)
            rw, sel = jax.lax.top_k(scores, TOPK)
            rw = rw / jnp.sum(rw, axis=-1, keepdims=True)
            routing_mask = jax.nn.one_hot(sel, E, dtype=jnp.int32).sum(2)
            s_eff = s * TOPK
            xr = jnp.repeat(x, TOPK, axis=1).reshape(b * s_eff, d)
            batch_idx = jnp.repeat(jnp.arange(b), s_eff)
            combined = batch_idx * E + sel.reshape(-1)
            sorted_indices = jnp.argsort(combined)
            x_sorted = xr[sorted_indices]
            counts = routing_mask.sum(1)
            flat_end = (jnp.cumsum(counts, axis=1) + jnp.arange(b)[:, None] * s_eff).reshape(-1)
            start = jnp.concatenate([jnp.zeros((1,), flat_end.dtype), flat_end[:-1]])
            pos = jnp.arange(CAP)[None, :] + start[:, None]
            trunc = pos + counts.reshape(-1)[:, None] - CAP
            mask = (trunc < flat_end[:, None]) & (trunc >= 0) & (trunc >= start[:, None])
            trunc = jnp.where(mask, trunc, 0)
            xe = x_sorted[trunc.reshape(-1)].reshape(b * E, CAP, d) * mask[..., None]
            xe = xe.reshape(b, E, CAP, d).transpose(1, 0, 2, 3)
            q = jnp.einsum('ebtd,kd->ebtk', xe, Wq).reshape(E, b, CAP, HEADS, HEAD_K)
            k = jnp.einsum('ebtd,ekd->ebtk', xe, Wk).reshape(E, b, CAP, HEADS, HEAD_K)
            v = jnp.einsum('ebtd,ekd->ebtk', xe, Wv).reshape(E, b, CAP, HEADS, HEAD_V)
            f = jnp.einsum('ebtd,ekd->ebtk', xe, Wf).reshape(E, b, CAP, HEADS, NSLOTS)
            g = jax.nn.log_sigmoid(f) / GATE_NORM
            slot = 1.0 - jnp.exp(g)
            q, k = (swish(q), swish(k))
            tr = lambda a: a.transpose(0, 1, 3, 2, 4)
            o = gsa_chunk(tr(q), tr(k), tr(v), tr(slot), tr(g)).transpose(0, 1, 3, 2, 4)
            gathered = o.transpose(1, 0, 2, 3, 4).reshape(b * E * CAP, HEADS, HEAD_V)
            gathered = gathered * mask.reshape(-1)[:, None, None]
            resort = jnp.zeros((b * s_eff, HEADS, HEAD_V), gathered.dtype).at[trunc.reshape(-1)].add(gathered)
            restored = resort[jnp.argsort(sorted_indices)].reshape(b, s, TOPK, HEADS, HEAD_V)
            out = (restored * rw[..., None, None]).sum(2).reshape(b, s, HIDDEN)
            return jnp.einsum('bsd,od->bso', rms_norm(out, gnorm_w), Wo)
        return forward(hidden_states, norm_w, Wg, Wq, Wk, Wv, Wf, gnorm_w, Wo)
    x = x + _L0_xattn_ref(ctx_1024, ctx_1024, _layernorm(x, axis=-1), L0_xattn_Wk, L0_xattn_Wv, L0_xattn_bv, L0_xattn_Wq, L0_xattn_bq, L0_xattn_Wo, L0_xattn_bo)
    x = x + _L0_ffn_ref(_layernorm(x, axis=-1), L0_ffn_norm_w, L0_ffn_Wg, L0_ffn_Wq, L0_ffn_Wk, L0_ffn_Wv, L0_ffn_Wf, L0_ffn_gnorm_w, L0_ffn_Wo)
    return x

_drawn_inputs = setup_inputs


def setup_inputs(seed=0):
    import zlib

    import numpy as np

    out = dict(_drawn_inputs(seed))
    spreads = {'L0_xattn_bv': (0.0, 0.1),
     'L0_xattn_bq': (0.0, 0.1),
     'L0_xattn_bo': (0.0, 0.1),
     'L0_ffn_norm_w': (1.0, 0.2),
     'L0_ffn_gnorm_w': (1.0, 0.2)}
    factors = {'L0_ffn_Wq': 8.0, 'L0_ffn_Wk': 8.0, 'L0_ffn_Wf': 8.0}
    for name, (base, spread) in spreads.items():
        noise = np.random.default_rng([zlib.crc32(name.encode()), seed]).standard_normal(out[name].shape)
        drawn = base * np.exp(spread * noise) if base else spread * noise
        out[name] = jnp.asarray(drawn.astype(out[name].dtype))
    for name, factor in factors.items():
        out[name] = (out[name] * factor).astype(out[name].dtype)
    return out
```

```python
from contextlib import ExitStack

import concourse.bass as bass
from concourse import mybir

ALU = mybir.AluOpType
ACT = mybir.ActivationFunctionType
F32 = mybir.dt.float32
I32 = mybir.dt.int32
AX = mybir.AxisListType.X

P = 128
B, T, D = 32, 256, 256
K = 77
E, HEADS, HD = 8, 4, 64
TPB = T // P
KT = D // P
NT = B * T // P
EPS = 1e-5
ISQ = D ** -0.5
GN = 1.0 / 8.0

REG = B * T + P
NCH = 2 * B * T // P + E
PADROW = E * REG
RW = 2 * D + 4
CB_, CN_, CE_, CU_ = 2 * D, 2 * D + 1, 2 * D + 2, 2 * D + 3
NOUT = 3 * B * T + P


def wait(eng, sem, count):
    if isinstance(count, int) and count <= 0:
        return
    eng.wait_ge(sem, count)


def turns(eng, first, lo, hi, last, body):
    for b in range(first, lo):
        body(b, b % 2)
    with eng.Fori(lo // 2, hi // 2) as i:
        for u in range(2):
            body(i * 2 + u, u)
    for b in range(hi, last):
        body(b, b % 2)


def hold(eng, sem):
    eng.sem_inc(sem, 1)


def within(b, lo, hi):
    return not isinstance(b, int) or lo <= b < hi


def xattn_gsa_moe(nc, x, ctxT, wk, wq, wv, woT, bqc, bvc, bo, nwc, wqgT, wfkvT, gwc, fwoT, out):
    with ExitStack() as ctx:
        def sb(name, shape, dt=F32):
            return ctx.enter_context(nc.sbuf_tensor(name, shape, dt))

        S = {}

        def sem(*names):
            for n in names:
                S[n] = ctx.enter_context(nc.semaphore(n))

        rows_d = nc.dram_tensor("rows_d", [PADROW + E * P, RW], F32).ap()
        exp_d = nc.dram_tensor("exp_d", [NOUT, D], F32).ap()

        ps = ctx.enter_context(nc.psum_tensor("ps", [P, 8, 512], F32))

        X1 = sb("X1", [P, NT, D])
        W = sb("W", [P, E, KT * 3 * D])
        GW = sb("GW", [P, KT, D])
        ident = sb("ident", [P, P])
        triM = sb("triM", [P, P])
        triS = sb("triS", [P, P])
        cumT = sb("cumT", [P, P])
        halves = sb("halves", [P, 2])
        ones = sb("ones", [P, P])
        mhalf = sb("mhalf", [P, 2])
        nidx = sb("nidx", [P, NT])
        bidx = sb("bidx", [P, NT])
        D21 = sb("D21", [P, NT])
        RW1 = sb("RW1", [P, NT])
        RW2 = sb("RW2", [P, NT])
        RWT = sb("RWT", [P, NT])
        vtmp = sb("vtmp", [P, 3, KT])
        gcol = sb("gcol", [P, KT])
        PADR = sb("PADR", [P, RW])
        BASE = sb("BASE", [P, 2, TPB, E])
        eoff = sb("eoff", [P, E])
        cio = sb("cio", [P, NCH])
        keep, phase = ctx, ExitStack()
        ctx = phase
        wtmp = sb("wtmp", [P, 4, KT, D])
        M1 = sb("M1", [P, KT, D])
        M2 = sb("M2", [P, KT, D])
        wb = sb("wb", [P, KT])
        CBc = sb("CBc", [P, D])
        bob = sb("bob", [P, D])
        WQG = sb("WQG", [P, KT, D + E])
        wrev = sb("wrev", [P, TPB, E])
        CTX = sb("CTX", [P, 2, KT, K])
        KQ = sb("KQ", [P, 2, 3, K])
        VO = sb("VO", [K, 2, D])
        BN1 = sb("BN1", [P, TPB, 6])
        MV1 = sb("MV1", [P, 2, TPB, 2])
        VE1 = sb("VE1", [P, 2, TPB])
        RS1 = sb("RS1", [P, 2, TPB])
        XN = sb("XN", [P, TPB, D])
        XNT = sb("XNT", [P, TPB, KT, P])
        SS = sb("SS", [P, TPB, K])
        MX = sb("MX", [P, TPB])
        SM = sb("SM", [P, TPB, K])
        PR = sb("PR", [P, TPB, K])
        SUM = sb("SUM", [P, 2, TPB])
        RI = sb("RI", [P, TPB])
        PT = sb("PT", [K, 2, TPB, P])
        BN2 = sb("BN2", [P, TPB, 6])
        MV2 = sb("MV2", [P, 2, TPB, 2])
        VE2 = sb("VE2", [P, 2, TPB])
        CO2 = sb("CO2", [P, 2, TPB])
        ROW = sb("ROW", [P, 2, TPB, RW])
        YT = sb("YT", [P, TPB, KT, P])
        AQ = sb("AQ", [P, TPB, D])
        EQ = sb("EQ", [P, TPB, D])
        LQ = sb("LQ", [P, TPB, D])
        M1v = sb("M1v", [P, TPB])
        M2v = sb("M2v", [P, TPB])
        EQ1 = sb("EQ1", [P, TPB, E])
        KEY = sb("KEY", [P, 2, TPB])
        SEL = sb("SEL", [P, 2, TPB, E])
        L2 = sb("L2", [P, TPB, E])
        LG = sb("LG", [P, TPB, E])
        MASK = sb("MASK", [P, TPB, E])
        POS = sb("POS", [P, TPB, E])
        POSK = sb("POSK", [P, 2, TPB, E])
        IDF = sb("IDF", [P, 2, TPB])
        IDX = sb("IDX", [P, 2, 2 * TPB], I32)
        phase.close()
        ctx = keep
        CNTI = sb("CNTI", [P, E], I32)
        NCI = sb("NCI", [P, E], I32)
        NCF = sb("NCF", [P, E])
        CEND = sb("CEND", [P, E])
        COEF = sb("COEF", [P, E])
        GE = sb("GE", [P, E, NCH])
        ECOL = sb("ECOL", [P, NCH])
        ECOLB = sb("ECOLB", [P, NCH])
        RTAB = sb("RTAB", [P, NCH])
        ETI = sb("ETI", [P, NCH], I32)
        RTI = sb("RTI", [P, NCH], I32)
        PDF = sb("PDF", [P, E])
        PDI = sb("PDI", [P, E], I32)
        X = sb("X", [P, 2, RW])
        META = sb("META", [P, 2, 4])
        IDO = sb("IDO", [P, 2, 1], I32)
        XT = sb("XT", [P, 2, 4, P])
        AB = sb("AB", [P, 2 * D])
        EX = sb("EX", [P, 2 * D])
        LN_ = sb("LN_", [P, 2 * D])
        LS = sb("LS", [P, 2, 2 * D])
        SG = sb("SG", [P, D])
        EG = sb("EG", [P, D])
        KV = sb("KV", [P, 2, 2, HEADS, HD])
        DEC = sb("DEC", [P, 2, D])
        EN = sb("EN", [P, D])
        EF = sb("EF", [P, 2, 2, 2])
        SIN = sb("SIN", [P, 2, D])
        SLA = sb("SLA", [P, 2, D])
        SINT = sb("SINT", [P, 2, 2, P])
        KTt = sb("KTt", [P, 2, P])
        MSK = sb("MSK", [P, 2, P])
        RM = sb("RM", [P, 2, P])
        SEGL = sb("SEGL", [P, 2, 1])
        CONT = sb("CONT", [P, 2, 1])
        FAC = sb("FAC", [P, 2, 2])
        AM = sb("AM", [P, 2, HEADS, P])
        QTM = sb("QTM", [P, 2, 2, P])
        SP_ = sb("SP_", [P, 2, 2, 2, 2, HD])
        ST = sb("ST", [P, 2, 2, 2, HD])
        HK = sb("HK", [P, 2, 2, P])
        OKD = sb("OKD", [P, D])
        MXO = sb("MXO", [P, HEADS])
        SBO = sb("SBO", [P, D])
        EO = sb("EO", [P, D])
        SMO = sb("SMO", [P, HEADS])
        RIN = sb("RIN", [P, 2, HEADS])
        QVG = sb("QVG", [P, D])
        QVGT = sb("QVGT", [P, 2, P])
        QVM = sb("QVM", [P, 2, P])
        TM = sb("TM", [P, HEADS, P])
        OV = sb("OV", [P, 2, D])
        OC = sb("OC", [P, 2, 2, TPB, D])
        OS = sb("OS", [P, TPB, D])
        OM = sb("OM", [P, TPB, D])
        SQ = sb("SQ", [P, TPB])
        SQS = sb("SQS", [P, D])
        VE3 = sb("VE3", [P, TPB])
        RS3 = sb("RS3", [P, 2, TPB])
        OT = sb("OT", [P, TPB, KT, P])
        FO = sb("FO", [P, 2, TPB, D])

        sem("d_w0", "d_w1", "d_W", "d_x0", "d_x1", "d_c0", "d_c1", "d_pad", "d_scat0", "d_scat1", "d_padw",
            "d_row0", "d_row1", "d_o0", "d_o1", "d_oc0", "d_oc1", "d_out0", "d_out1")
        sem("iota", "cmem", "csel", "cumT", "halves", "foldq", "foldw", "foldg", "m_ps", "m1", "m2", "wb", "cb")
        sem("bn1", "stat1", "ve1", "rstd1", "xn", "xnT_ps", "xnT", "kq_ps", "kq", "vo", "s_ps", "ss", "mx", "sm",
            "p", "sump", "pT_ps", "pT", "attn_ps", "ri", "x1", "bn2", "stat2", "ve2", "comb", "y", "yT_ps", "yT",
            "qg_ps", "aq", "eq", "lq", "lsq", "sgq", "rowq", "route", "r_l2", "lg",
            "r_mask", "r_meta", "rank_ps", "r_b2", "r_pos",
            "idx", "turn_pool", "turn_dve")
        sem("tab", "tables", "zero", "states0")
        sem("xT_ps", "xT", "fk_ps", "seg_ps", "v_ps", "ab", "ex", "ln", "ls", "sg", "eg", "kk", "vv", "g_ps", "f_ps",
            "dec", "en", "ef", "sin", "seg", "last", "sla", "sinT_ps", "sinT", "kT_ps", "kT", "msk", "rm", "segl",
            "cont", "fac", "a_ps", "am", "qtm", "h_ps", "sp", "st", "hk_ps", "hk", "ok_ps", "okd", "mxo", "sbo",
            "eo", "smo", "rin", "qvg", "qvgT_ps", "qvgT", "qvm", "t_ps", "tm", "ov_ps", "ov", "ido")
        sem("seg2", "seg3", "rwd", "rwe", "rw", "om", "os", "sq", "ve3", "rs3", "osT_ps", "osT", "fo_ps", "fo")

        block = ctx.enter_context(nc.Block())

        def phase_a_over(eng):
            for name, per in (("attn_ps", 1), ("x1", 2), ("y", 1), ("yT", 1), ("qg_ps", 1), ("s_ps", 1), ("pT_ps", 1),
                              ("pT", 1), ("sump", 1), ("kq", 1), ("vo", 1), ("comb", 1), ("rstd1", 1), ("rowq", 1),
                              ("sgq", 1), ("idx", 1), ("xn", 1), ("xnT", 1), ("rank_ps", 1)):
                eng.wait_ge(S[name], per * B)
            for u in range(2):
                eng.wait_ge(S[f"d_scat{u}"], 64 * B // 2)

        @block.sync
        def _(sp):
            for i, w_ in enumerate((wk, wq, wv, woT)):
                sp.dma_start(wtmp[:, i], w_.rearrange("(k p) n -> p k n", p=P)).then_inc(S["d_w0"], 16)
            sp.dma_start(vtmp[:, 0], bqc).then_inc(S["d_w0"], 16)
            sp.dma_start(vtmp[:, 1], bvc).then_inc(S["d_w0"], 16)
            sp.dma_start(bob[:, :], bo.partition_broadcast(P)).then_inc(S["d_w0"], 16)
            sp.dma_start(vtmp[:, 2], nwc).then_inc(S["d_w1"], 16)
            sp.dma_start(gcol[:, :], gwc).then_inc(S["d_w1"], 16)
            sp.dma_start(WQG[:, :, :], wqgT.rearrange("(k p) n -> p k n", p=P)).then_inc(S["d_w1"], 16)
            sp.dma_start(GW[:, :, :], fwoT.rearrange("(k p) n -> p k n", p=P)).then_inc(S["d_w1"], 16)
            before, ready = sp.alloc_register("before"), sp.alloc_register("ready")

            def load(b, u):
                if isinstance(b, int):
                    nb, nr = b - 1, 8 * (b - u)
                else:
                    sp.reg_add(before, b, -1)
                    sp.reg_mul(ready, b - u, 8)
                    nb, nr = before, ready
                wait(sp, S["kq_ps"], nb)
                wait(sp, S["d_x0" if u == 0 else "d_x1"], nr)
                sp.dma_start(X1[:, bass.ds(b * TPB, TPB), :],
                             x[bass.ds(b * T, T), :].rearrange("(t p) d -> p t d", p=P)).then_inc(S[f"d_x{u}"], 16)
                sp.dma_start(CTX[:, u], ctxT[bass.ds(b * D, D), :].rearrange("(k p) n -> p k n", p=P))\
                    .then_inc(S[f"d_c{u}"], 16)

            turns(sp, 0, 4, B - 2, B, load)
            sp.wait_ge(S["zero"], 3)
            for i in range(E):
                sp.dma_start(rows_d[PADROW + i * P:PADROW + (i + 1) * P, :], PADR[:, :]).then_inc(S["d_pad"], 16)
            sp.wait_ge(S["tables"], 1)
            phase_a_over(sp)
            for e in range(E):
                r = sp.value_load(PDI[0:1, e:e + 1], min_val=0, max_val=PADROW)
                sp.dma_start(rows_d[bass.ds(r, P), :], PADR[:, :]).then_inc(S["d_padw"], 16)
            sp.wait_ge(S["d_pad"], 16 * E)
            sp.wait_ge(S["d_padw"], 16 * E)
            used = sp.alloc_register("used")

            def row(c, u):
                if isinstance(c, int):
                    nu = c - 1
                else:
                    sp.reg_add(used, c, -1)
                    nu = used
                r = sp.value_load(RTI[0:1, bass.ds(c, 1)], min_val=0, max_val=PADROW + (E - 1) * P)
                wait(sp, S["seg_ps"], nu)
                wait(sp, S["msk"], nu)
                wait(sp, S["ido"], nu)
                wait(sp, S["xT_ps"], nu)
                sp.dma_start(X[:, u, :], rows_d[bass.ds(r, P), :]).then_inc(S[f"d_row{u}"], 16)

            turns(sp, 0, 4, NCH - 2, NCH, row)
            sp.wait_ge(S["d_o0"], 16 * NCH // 2)
            sp.wait_ge(S["d_o1"], 16 * NCH // 2)

            def pair(b, u):
                if isinstance(b, int):
                    nu = b - 1
                else:
                    sp.reg_add(used, b, -1)
                    nu = used
                wait(sp, S["os"], nu)
                for k in range(2):
                    sp.dma_start(OC[:, u, k], exp_d[bass.ds(b * T + k * B * T, T), :]
                                 .rearrange("(t p) d -> p t d", p=P)).then_inc(S[f"d_oc{u}"], 16)

            turns(sp, 0, 4, B - 2, B, pair)

        @block.gpsimd
        def _(g):
            i_ = lambda t, pat, base, cm: nc.gpsimd.iota(t, pat, base=base, channel_multiplier=cm,
                                                         allow_small_or_imprecise_dtypes=True).then_inc(S["iota"], 1)
            g.memset(ident[:, :], 0.0).then_inc(S["cmem"], 1)
            g.memset(triM[:, :], 1.0).then_inc(S["cmem"], 1)
            g.memset(triS[:, :], 1.0).then_inc(S["cmem"], 1)
            g.memset(cumT[:, :], GN).then_inc(S["cmem"], 1)
            g.memset(ones[:, :], 1.0).then_inc(S["cmem"], 1)
            g.memset(mhalf[:, :], -0.5).then_inc(S["cmem"], 1)
            g.wait_ge(S["cmem"], 6)
            sel = lambda t, op, cm, st, fill: g.affine_select(
                out=t, in_=t, compare_op=op, fill=fill, base=0, pattern=[[st, P]], channel_multiplier=cm)\
                .then_inc(S["csel"], 1)
            sel(ident[:, :], ALU.not_equal, 1, -1, 1.0)
            i_(wrev[:, :, :], [[0, TPB], [-1, E]], E, 0)
            i_(eoff[:, :], [[REG, E]], 0, 0)
            i_(nidx[:, :], [[P, NT]], B * T, 1)
            i_(bidx[:, :], [[1, B], [0, TPB]], 0, 0)
            i_(cio[:, :], [[1, NCH]], 0, 0)
            sel(triM[:, :], ALU.is_ge, -1, 1, 0.0)
            sel(triS[:, :], ALU.is_gt, -1, 1, 0.0)
            sel(cumT[:, :], ALU.is_ge, -1, 1, 0.0)
            g.memset(PADR[:, :], 0.0).then_inc(S["zero"], 1)
            g.wait_ge(S["zero"], 1)
            g.memset(PADR[:, CB_:CB_ + 1], -0.5).then_inc(S["zero"], 1)
            i_(PADR[:, CN_:CN_ + 1], [[0, 1]], 3 * B * T, 1)
            g.memset(ROW[:, :, :, CU_:CU_ + 1], 0.0).then_inc(S["cmem"], 1)
            g.wait_ge(S["iota"], 6)
            g.wait_ge(S["zero"], 2)
            g.wait_ge(S["cmem"], 7)
            g.memset(PADR[:, CU_:CU_ + 1], 0.0).then_inc(S["zero"], 1)

            def batch(b, u):
                if within(b, -1, B - 1):
                    v = 1 - u
                    wait(g, S["stat2"], b + 2)
                    wait(g, S["y"], b)
                    hold(g, S["turn_pool"])
                    g.tensor_scalar(VE2[:, v, :], MV2[:, v, :, 1], 1.0 + EPS, EPS * EPS, ALU.mult, ALU.add)\
                        .then_inc(S["ve2"], 1)
                    wait(g, S["ve2"], b + 2)
                    g.tensor_tensor(CO2[:, v, :], VE2[:, v, :], mhalf[:, :], ALU.pow).then_inc(S["comb"], 1)
                if within(b, -2, B - 2):
                    wait(g, S["stat1"], b + 3)
                    wait(g, S["xn"], b + 1)
                    hold(g, S["turn_pool"])
                    g.tensor_scalar(VE1[:, u, :], MV1[:, u, :, 1], 1.0, EPS, ALU.mult, ALU.add)\
                        .then_inc(S["ve1"], 1)
                    wait(g, S["ve1"], b + 3)
                    g.tensor_tensor(RS1[:, u, :], VE1[:, u, :], mhalf[:, :], ALU.pow).then_inc(S["rstd1"], 1)
                if within(b, 0, B):
                    wait(g, S["idx"], b + 1)
                    wait(g, S["rowq"], b + 1)
                    wait(g, S["r_meta"], 2 * b + 2)
                    hold(g, S["turn_pool"])
                    for k in range(2):
                        for t in range(TPB):
                            g.indirect_dma_start(rows_d, bass.IndirectOffsetOnAxis(
                                ap=IDX[:, u, k * TPB + t:k * TPB + t + 1], axis=0), ROW[:, u, t, :], None)\
                                .then_inc(S[f"d_scat{u}"], 16)

            turns(g, -2, 4, B - 2, B, batch)

            def chunk(c, u):
                n, v = c + 1, 1 - u
                s1, s2 = within(c, -1, NCH - 1), within(c, 0, NCH)
                if s1:
                    wait(g, S[f"d_row{v}"], 8 * (n - v) + 16)
                    wait(g, S["msk"], n - 1)
                    hold(g, S["turn_pool"])
                    g.tensor_tensor(META[:, v, 0:1], ECOLB[:, bass.ds(n, 1)], X[:, v, CB_:CB_ + 1], ALU.add)\
                        .then_inc(S["seg"], 1)
                    g.tensor_tensor(META[:, v, 1:2], ECOL[:, bass.ds(n, 1)], X[:, v, CE_:CE_ + 1], ALU.subtract)\
                        .then_inc(S["seg2"], 1)
                    wait(g, S["seg2"], n + 1)
                    hold(g, S["turn_pool"])
                    g.tensor_scalar(META[:, v, 2:3], META[:, v, 1:2], 0.0, -float(B * T), ALU.is_equal, ALU.mult)\
                        .then_inc(S["seg3"], 1)
                    wait(g, S["seg3"], 2 * n + 1)
                    g.tensor_tensor(META[:, v, 1:2], META[:, v, 2:3], X[:, v, CN_:CN_ + 1], ALU.add)\
                        .then_inc(S["seg3"], 1)
                    wait(g, S["seg3"], 2 * n + 2)
                    wait(g, S[f"d_o{v}"], 8 * (n - v))
                    hold(g, S["turn_pool"])
                    g.tensor_copy(IDO[:, v, :], META[:, v, 1:2])\
                        .then_inc(S["ido"], 1)
                    wait(g, S["segl"], n + 2)
                    wait(g, S["st"], 2 * n - 2)
                    hold(g, S["turn_pool"])
                    g.tensor_scalar(META[:, v, 3:4], META[:, v, 0:1], SEGL[:, v, :], 1.0, ALU.is_equal, ALU.mult)\
                        .then_inc(S["last"], 1)
                    g.tensor_scalar(CONT[:, v, :], SEGL[:, u, :], SEGL[:, v, :], 1.0, ALU.is_equal, ALU.mult)\
                        .then_inc(S["cont"], 1)
                    wait(g, S["rm"], n + 1)
                    wait(g, S["xT"], n + 1)
                    wait(g, S["ok_ps"], n - 1)
                    g.tensor_tensor(QTM[:, v], XT[:, v, 2:4, :],
                                    RM[:, v].unsqueeze(1).broadcast_to([P, 2, P]), ALU.mult).then_inc(S["qtm"], 1)
                if s2:
                    wait(g, S["qvgT"], c + 1)
                    wait(g, S["ov_ps"], c)
                    g.tensor_tensor(QVM[:, :, :], QVGT[:, :, :],
                                    RM[:, u].unsqueeze(1).broadcast_to([P, 2, P]), ALU.mult).then_inc(S["qvm"], 1)
                if s1:
                    wait(g, S["ef"], n + 2)
                    wait(g, S["sp"], n - 1)
                    g.tensor_tensor(FAC[:, v, :], EF[:, u, :, 1], EF[:, v, :, 0], ALU.mult).then_inc(S["fac"], 1)
                    wait(g, S["sin"], n + 1)
                    wait(g, S["last"], n + 1)
                    wait(g, S["h_ps"], n - 1)
                    hold(g, S["turn_pool"])
                    g.tensor_scalar(SLA[:, v], SIN[:, v], META[:, v, 3:4], 1.0, ALU.mult, ALU.mult)\
                        .then_inc(S["sla"], 1)
                if s2:
                    wait(g, S["ov"], c + 1)
                    wait(g, S["ido"], c + 1)
                    wait(g, S[f"d_o{v}"], 8 * (c + 1 - v))
                    hold(g, S["turn_pool"])
                    g.indirect_dma_start(exp_d, bass.IndirectOffsetOnAxis(ap=IDO[:, u, :], axis=0),
                                         OV[:, u, :], None).then_inc(S[f"d_o{u}"], 16)

            phase_a_over(g)
            g.wait_ge(S["tables"], 1)
            g.wait_ge(S["segl"], 1)
            g.wait_ge(S["ef"], 1)
            turns(g, -1, 4, NCH - 2, NCH, chunk)

            def final(b, u):
                wait(g, S["sq"], 2 * b + 2)
                wait(g, S["rs3"], b)
                hold(g, S["turn_pool"])
                g.tensor_scalar(VE3[:, :], SQ[:, :], 1.0 / D, EPS, ALU.mult, ALU.add).then_inc(S["ve3"], 1)
                wait(g, S["ve3"], b + 1)
                wait(g, S["fo"], 2 * b - 2)
                g.tensor_tensor(RS3[:, u, :], VE3[:, :], mhalf[:, :], ALU.pow).then_inc(S["rs3"], 1)

            turns(g, 0, 4, B - 2, B, final)

        @block.tensor
        def _(pe):
            mm = nc.tensor.matmul
            tr = lambda o, i, n=P: nc.tensor.transpose(o, i, ident[0:n, 0:n])
            pe.wait_ge(S["d_w0"], 16 * 7)
            pe.wait_ge(S["csel"], 1)
            for i, (l, r) in enumerate(((0, 1), (2, 3))):
                for cb in range(KT):
                    for eb in range(KT):
                        last = mm(ps[:, i, cb * D:(cb + 1) * D], wtmp[:, l, eb, cb * P:(cb + 1) * P],
                                  wtmp[:, r, eb, :], start=(eb == 0), stop=(eb == KT - 1))
            for cb in range(KT):
                for eb in range(KT):
                    mm(ps[:, 2, cb:cb + 1], wtmp[:, 0, eb, cb * P:(cb + 1) * P], vtmp[:, 0, eb:eb + 1],
                       start=(eb == 0), stop=(eb == KT - 1))
            for eb in range(KT):
                last = mm(ps[:, 3, 0:D], vtmp[:, 1, eb:eb + 1].broadcast_to([P, P]), wtmp[:, 3, eb, :],
                          start=(eb == 0), stop=(eb == KT - 1))
            last.then_inc(S["m_ps"], 1)
            pe.wait_ge(S["m1"], 1)
            pe.wait_ge(S["m2"], 1)
            pe.wait_ge(S["wb"], 1)
            pe.wait_ge(S["cb"], 1)

            def batch(b, u):
                a1, a2, a3 = within(b, -2, B - 2), within(b, -1, B - 1), within(b, 0, B)
                v = 1 - u
                if a2:
                    wait(pe, S["pT"], b + 2)
                    wait(pe, S["vo"], b + 2)
                    wait(pe, S["x1"], 2 * b + 2)
                    for t in range(TPB):
                        last = mm(ps[:, 2, t * D:(t + 1) * D], PT[:, v, t, :], VO[:, v, :], start=True, stop=True)
                    last.then_inc(S["attn_ps"], 1)
                if a1:
                    wait(pe, S[f"d_c{u}"], 8 * (b + 2 - u) + 16)
                    wait(pe, S["kq"], b + 2)
                    wait(pe, S["vo"], b + 2)
                    for xb in range(KT):
                        for cb in range(KT):
                            mm(ps[:, 6, xb * K:(xb + 1) * K], M1[:, cb, xb * P:(xb + 1) * P], CTX[:, u, cb, :],
                               start=(cb == 0), stop=(cb == KT - 1))
                    for cb in range(KT):
                        mm(ps[:, 6, 2 * K:3 * K], wb[:, cb:cb + 1].broadcast_to([P, P]), CTX[:, u, cb, :],
                           start=(cb == 0), stop=(cb == KT - 1))
                    for cb in range(KT):
                        last = mm(ps[0:K, 6, 256:512], CTX[:, u, cb, :], M2[:, cb, :],
                                  start=(cb == 0), stop=(cb == KT - 1))
                    last.then_inc(S["kq_ps"], 1)
                if a3:
                    wait(pe, S["r_mask"], b + 1)
                    wait(pe, S["r_pos"], b)
                    mm(ps[:, 7, 0:TPB * E], triS[:, :], MASK[:, :, :], start=True, stop=True)
                    mm(ps[:, 7, TPB * E:2 * TPB * E], ones[:, :], MASK[:, :, :], start=True, stop=True)\
                        .then_inc(S["rank_ps"], 1)
                if a1:
                    wait(pe, S["xn"], b + 3)
                    wait(pe, S["xnT"], b + 2)
                    for t in range(TPB):
                        for k in range(KT):
                            last = tr(ps[:, 0, (t * KT + k) * P:(t * KT + k + 1) * P], XN[:, t, k * P:(k + 1) * P])
                    last.then_inc(S["xnT_ps"], 1)
                if a2:
                    wait(pe, S["y"], b + 2)
                    wait(pe, S["yT"], b + 1)
                    for t in range(TPB):
                        for k in range(KT):
                            last = tr(ps[:, 3, (t * KT + k) * P:(t * KT + k + 1) * P],
                                      ROW[:, v, t, k * P:(k + 1) * P])
                    last.then_inc(S["yT_ps"], 1)
                if a1:
                    wait(pe, S["xnT"], b + 3)
                    wait(pe, S["kq"], b + 3)
                    wait(pe, S["pT"], b + 2)
                    for t in range(TPB):
                        for k in range(KT):
                            last = mm(ps[:, 1, t * K:(t + 1) * K], XNT[:, t, k, :], KQ[:, u, k, :],
                                      start=(k == 0), stop=(k == KT - 1))
                    last.then_inc(S["s_ps"], 1)
                if a2:
                    wait(pe, S["yT"], b + 2)
                    wait(pe, S["foldq"], 2)
                    wait(pe, S["rowq"], b + 1)
                    wait(pe, S["r_l2"], b + 1)
                    for t in range(TPB):
                        for k in range(KT):
                            last = mm(ps[:, 4 + t, 0:D + E], YT[:, t, k, :], WQG[:, k, :],
                                      start=(k == 0), stop=(k == KT - 1))
                    last.then_inc(S["qg_ps"], 1)
                if a1:
                    wait(pe, S["p"], b + 3)
                    wait(pe, S["pT"], b + 2)
                    for t in range(TPB):
                        last = tr(ps[0:K, 1, 256 + t * P:256 + (t + 1) * P], PR[:, t, :])
                    last.then_inc(S["pT_ps"], 1)

            turns(pe, -2, 4, B - 2, B, batch)
            pe.wait_ge(S["tables"], 1)
            pe.wait_ge(S["csel"], 4)
            pe.wait_ge(S["cumT"], 1)
            pe.wait_ge(S["foldw"], 2)
            pe.wait_ge(S["states0"], 2)
            pe.wait_ge(S["halves"], 4)

            def rows_transposed(m, w):
                wait(pe, S[f"d_row{w}"], 8 * (m - w) + 16)
                wait(pe, S["xT"], m)
                for k in range(4):
                    last = tr(ps[:, 2, k * P:(k + 1) * P], X[:, w, k * P:(k + 1) * P])
                last.then_inc(S["xT_ps"], 1)

            def chunk(c, u):
                n, v = c + 1, 1 - u
                s1, s2 = within(c, -1, NCH - 1), within(c, 0, NCH)
                if s1:
                    e = pe.value_load(ETI[0:1, bass.ds(n, 1)], min_val=0, max_val=E - 1)
                if s2:
                    wait(pe, S["am"], c + 1)
                    wait(pe, S["qtm"], c + 1)
                    wait(pe, S["hk"], c + 1)
                    for pr in range(2):
                        mm(ps[:, 4, 256 + pr * P:256 + (pr + 1) * P], QTM[:, u, pr, :], HK[:, u, pr, :],
                           start=True, stop=True)
                        for h in (2 * pr, 2 * pr + 1):
                            last = mm(ps[:, 4, 256 + h * HD:256 + (h + 1) * HD], AM[:, u, h, :],
                                      SIN[:, u, h * HD:(h + 1) * HD], start=False, stop=True,
                                      skip_group_check=True)
                    last.then_inc(S["ok_ps"], 1)
                if s1:
                    wait(pe, S["xT"], n + 1)
                    wait(pe, S["kk"], n)
                    for k in range(KT):
                        last = mm(ps[:, 0, :], XT[:, v, k, :],
                                  W[:, bass.ds(e, 1), k * 3 * D:k * 3 * D + 2 * D].rearrange("p a n -> p (a n)"),
                                  start=(k == 0), stop=(k == KT - 1))
                    last.then_inc(S["fk_ps"], 1)
                    wait(pe, S["seg"], n + 1)
                    wait(pe, S["segl"], n)
                    wait(pe, S["rm"], n)
                    wait(pe, S["ef"], n + 1)
                    tr(ps[:, 3, 0:P], META[:, v, 0:1].broadcast_to([P, P])).then_inc(S["seg_ps"], 1)
                    wait(pe, S["vv"], n)
                    wait(pe, S["dec"], n)
                    for k in range(KT):
                        last = mm(ps[:, 1, 0:D], XT[:, v, k, :],
                                  W[:, bass.ds(e, 1), k * 3 * D + 2 * D:(k + 1) * 3 * D]
                                  .rearrange("p a n -> p (a n)"), start=(k == 0), stop=(k == KT - 1))
                    last.then_inc(S["v_ps"], 1)
                if s2:
                    wait(pe, S["qvg"], c + 1)
                    if s1:
                        wait(pe, S["rm"], n + 1)
                    for pr in range(2):
                        last = tr(ps[:, 3, 256 + pr * P:256 + (pr + 1) * P], QVG[:, pr * P:(pr + 1) * P])
                    last.then_inc(S["qvgT_ps"], 1)
                if within(c, -1, NCH - 2):
                    rows_transposed(n + 1, u)
                if s2:
                    wait(pe, S["qvgT"], c + 1)
                    wait(pe, S["sinT"], c + 1)
                    for h in range(HEADS):
                        q = slice(HD * (h % 2), HD * (h % 2) + HD)
                        last = mm(ps[:, 4 + h % 2, (h // 2) * P:(h // 2 + 1) * P], SINT[q, u, h // 2, :],
                                  QVGT[q, h // 2, :], start=True, stop=True)
                    last.then_inc(S["t_ps"], 1)
                if s1:
                    wait(pe, S["ls"], n + 1)
                    wait(pe, S["vv"], n + 1)
                    wait(pe, S["en"], n)
                    wait(pe, S["ef"], n)
                    mm(ps[:, 1, 256:512], cumT[:, :], LS[:, v, 0:D], start=True, stop=True).then_inc(S["g_ps"], 1)
                    for pr in range(2):
                        last = mm(ps[:, 3, 128 + 2 * pr:130 + 2 * pr], LS[:, v, pr * P:(pr + 1) * P], halves[:, :],
                                  start=True, stop=True)
                    last.then_inc(S["f_ps"], 1)
                if s2:
                    wait(pe, S["tm"], c + 1)
                    wait(pe, S["qvm"], c + 1)
                    wait(pe, S["sp"], c + 1)
                    for pr in range(2):
                        mm(ps[:, 5, 256 + pr * P:256 + (pr + 1) * P], QVM[:, pr, :], SP_[:, u, pr, 1, :, :],
                           start=True, stop=True)
                        for h in (2 * pr, 2 * pr + 1):
                            last = mm(ps[:, 5, 256 + h * HD:256 + (h + 1) * HD], TM[:, h, :], KV[:, u, 1, h, :],
                                      start=False, stop=True, skip_group_check=True)
                    last.then_inc(S["ov_ps"], 1)
                if s1:
                    wait(pe, S["kk"], n + 1)
                    wait(pe, S["sinT"], n)
                    for pr in range(2):
                        last = tr(ps[:, 6, pr * P:(pr + 1) * P], KV[:, v, 0, 2 * pr:2 * pr + 2, :])
                    last.then_inc(S["kT_ps"], 1)
                    wait(pe, S["sp"], n + 1)
                    wait(pe, S["hk"], n)
                    for pr in range(2):
                        last = tr(ps[:, 7, 256 + pr * P:256 + (pr + 1) * P], SP_[:, v, pr, 0, :, :])
                    last.then_inc(S["hk_ps"], 1)
                    wait(pe, S["kT"], n + 1)
                    wait(pe, S["sin"], n + 1)
                    for pr in range(2):
                        last = tr(ps[:, 6, 256 + pr * P:256 + (pr + 1) * P], SIN[:, v, pr * P:(pr + 1) * P])
                    last.then_inc(S["sinT_ps"], 1)
                    wait(pe, S["ov"], c + 1)
                    for h in range(HEADS):
                        q = slice(HD * (h % 2), HD * (h % 2) + HD)
                        last = mm(ps[:, 4 + h % 2, (h // 2) * P:(h // 2 + 1) * P], KTt[q, h // 2, :],
                                  XT[q, v, 2 + h // 2, :], start=True, stop=True)
                    last.then_inc(S["a_ps"], 1)
                    wait(pe, S["sla"], n + 1)
                    wait(pe, S["hk"], n + 1)
                    wait(pe, S["st"], 2 * n)
                    for h in range(HEADS):
                        q = slice(HD * (h % 2), HD * (h % 2) + HD)
                        last = mm(ps[q, 7, (h // 2) * P:(h // 2 + 1) * P], SLA[:, v, h * HD:(h + 1) * HD],
                                  KV[:, v, :, h, :], start=True, stop=True)
                    last.then_inc(S["h_ps"], 1)

            phase_a_over(pe)
            rows_transposed(0, 0)
            turns(pe, -1, 4, NCH - 2, NCH, chunk)
            pe.wait_ge(S["foldg"], 2)

            def final(b, u):
                if within(b, 0, B):
                    wait(pe, S["os"], b + 1)
                    wait(pe, S["osT"], b)
                    for t in range(TPB):
                        for k in range(KT):
                            last = tr(ps[:, 0, (t * KT + k) * P:(t * KT + k + 1) * P], OS[:, t, k * P:(k + 1) * P])
                    last.then_inc(S["osT_ps"], 1)
                    wait(pe, S["osT"], b + 1)
                    wait(pe, S["fo"], 2 * b - 2)
                    for t in range(TPB):
                        for k in range(KT):
                            last = mm(ps[:, 1 + u, t * D:(t + 1) * D], OT[:, t, k, :], GW[:, k, :],
                                      start=(k == 0), stop=(k == KT - 1))
                    last.then_inc(S["fo_ps"], 1)

            turns(pe, 0, 4, B - 2, B, final)

        @block.scalar
        def _(act):
            A = nc.scalar.activation
            act.preload_act_table_set("natural_log_exp_and_others")
            act.dma_start(W[:, :, :], wfkvT).then_inc(S["d_W"], 16)
            act.wait_ge(S["m_ps"], 1)
            A(M1[:, :, :], ps[:, 0, :].rearrange("p (k n) -> p k n", k=KT), ACT.Copy).then_inc(S["m1"], 1)
            A(wb[:, :], ps[:, 2, 0:KT], ACT.Copy).then_inc(S["wb"], 1)

            def batch(b, u):
                a1, a2, a3 = within(b, -2, B - 2), within(b, -1, B - 1), within(b, 0, B)
                if a1:
                    wait(act, S["kq_ps"], b + 3)
                    wait(act, S["s_ps"], b + 1)
                    wait(act, S["ss"], b + 1)
                    A(KQ[:, u], ps[:, 6, 0:3 * K].rearrange("p (a n) -> p a n", a=3), ACT.Copy).then_inc(S["kq"], 1)
                if a3:
                    wait(act, S["lg"], b + 1)
                    wait(act, S["eq"], b)
                    A(AQ[:, :, :], ps[:, 4:6, 0:D], ACT.Abs).then_inc(S["aq"], 1)
                    wait(act, S["aq"], b + 1)
                    wait(act, S["lq"], b)
                    A(EQ[:, :, :], AQ[:, :, :], ACT.Exp, scale=-1.0).then_inc(S["eq"], 1)
                    wait(act, S["eq"], b + 1)
                    wait(act, S["rowq"], b)
                    A(LQ[:, :, :], EQ[:, :, :], ACT.Ln, bias=1.0).then_inc(S["lq"], 1)
                if a1:
                    wait(act, S["xnT_ps"], b + 3)
                    wait(act, S["s_ps"], b + 2)
                    A(XNT[:, :, :, :], ps[:, 0, :].rearrange("p (t k n) -> p t k n", t=TPB, k=KT), ACT.Copy)\
                        .then_inc(S["xnT"], 1)
                if a2:
                    wait(act, S["yT_ps"], b + 2)
                    wait(act, S["qg_ps"], b + 1)
                    A(YT[:, :, :, :], ps[:, 3, :].rearrange("p (t k n) -> p t k n", t=TPB, k=KT), ACT.Copy)\
                        .then_inc(S["yT"], 1)
                if a3:
                    wait(act, S["lsq"], b + 1)
                    A(EQ[:, :, :], AQ[:, :, :], ACT.Exp).then_inc(S["sgq"], 1)
                if a1:
                    wait(act, S["sm"], b + 3)
                    wait(act, S["pT_ps"], b + 2)
                    wait(act, S["sump"], b + 2)
                    A(PR[:, :, :], SM[:, :, :], ACT.Exp, scale=ISQ).then_inc(S["p"], 1)
                    wait(act, S["pT_ps"], b + 3)
                    wait(act, S["attn_ps"], b + 1)
                    A(PT[:, u], ps[0:K, 1, 256:512].rearrange("p (t n) -> p t n", t=TPB), ACT.Copy)\
                        .then_inc(S["pT"], 1)

            turns(act, -2, 4, B - 2, B, batch)

            def rows_out(m, w):
                wait(act, S["xT_ps"], m + 1)
                wait(act, S["qtm"], m - 1)
                wait(act, S["a_ps"], m - 1)
                wait(act, S["v_ps"], m - 1)
                A(XT[:, w], ps[:, 2, :].rearrange("p (k n) -> p k n", k=4), ACT.Copy).then_inc(S["xT"], 1)

            def chunk(c, u):
                n, v = c + 1, 1 - u
                s1, s2 = within(c, -1, NCH - 1), within(c, 0, NCH)
                if s2:
                    wait(act, S["sbo"], c + 1)
                    wait(act, S["smo"], c)
                    wait(act, S["qvg"], c)
                    A(EO[:, :], SBO[:, :], ACT.Exp).then_inc(S["eo"], 1)
                if s1:
                    wait(act, S["fk_ps"], n + 1)
                    wait(act, S["ex"], n)
                    A(AB[:, :], ps[:, 0, :], ACT.Abs).then_inc(S["ab"], 1)
                    wait(act, S["ab"], n + 1)
                    wait(act, S["ln"], n)
                    A(EX[:, :], AB[:, :], ACT.Exp, scale=-1.0).then_inc(S["ex"], 1)
                    wait(act, S["ex"], n + 1)
                    wait(act, S["ls"], n)
                    A(LN_[:, :], EX[:, :], ACT.Ln, bias=1.0).then_inc(S["ln"], 1)
                    wait(act, S["v_ps"], n + 1)
                    wait(act, S["ov_ps"], n - 1)
                    wait(act, S["h_ps"], n - 1)
                    A(KV[:, v, 1, :, :], ps[:, 1, 0:D].rearrange("p (h d) -> p h d", h=HEADS), ACT.Copy)\
                        .then_inc(S["vv"], 1)
                if within(c, -1, NCH - 2):
                    rows_out(n + 1, u)
                if s1:
                    wait(act, S["ls"], n + 1)
                    wait(act, S["kk"], n)
                    A(SG[:, :], LS[:, v, D:2 * D], ACT.Exp).then_inc(S["sg"], 1)
                    wait(act, S["sin"], n)
                    A(EG[:, :], LS[:, v, 0:D], ACT.Exp, scale=GN).then_inc(S["eg"], 1)
                    wait(act, S["g_ps"], n + 1)
                    A(EN[:, :], ps[:, 1, 256:512], ACT.Exp, scale=-1.0).then_inc(S["en"], 1)
                    wait(act, S["qvg"], n - 1)
                    A(DEC[:, v], ps[:, 1, 256:512], ACT.Exp).then_inc(S["dec"], 1)
                    wait(act, S["f_ps"], n + 1)
                    wait(act, S["fac"], n)
                    A(EF[:, v], ps[:, 3, 128:132].rearrange("p (a b) -> p a b", a=2), ACT.Exp).then_inc(S["ef"], 1)
                    wait(act, S["fac"], n + 1)
                    wait(act, S["st"], 2 * n)
                    wait(act, S["ov_ps"], n - 1)
                    wait(act, S["hk_ps"], n - 1)
                    for pr in range(2):
                        last = A(SP_[:, v, pr], ST[:, pr], ACT.Copy, scale=FAC[:, v, pr:pr + 1])
                    last.then_inc(S["sp"], 1)
                    wait(act, S["kT_ps"], n + 1)
                    wait(act, S["a_ps"], n)
                    A(KTt[:, :, :], ps[:, 6, 0:256].rearrange("p (a n) -> p a n", a=2), ACT.Copy)\
                        .then_inc(S["kT"], 1)
                    wait(act, S["hk_ps"], n + 1)
                    wait(act, S["ok_ps"], n - 1)
                    A(HK[:, v], ps[:, 7, 256:512].rearrange("p (a n) -> p a n", a=2), ACT.Copy).then_inc(S["hk"], 1)
                    wait(act, S["sinT_ps"], n + 1)
                    wait(act, S["t_ps"], n - 1)
                    A(SINT[:, v], ps[:, 6, 256:512].rearrange("p (a n) -> p a n", a=2), ACT.Copy)\
                        .then_inc(S["sinT"], 1)

            phase_a_over(act)
            act.wait_ge(S["states0"], 2)
            rows_out(0, 0)
            turns(act, -1, 4, NCH - 2, NCH, chunk)
            act.wait_ge(S["r_meta"], 2 * B)
            A(RWT[:, :], D21[:, :], ACT.Exp).then_inc(S["rwe"], 1)

            def final(b, u):
                if within(b, 0, B):
                    wait(act, S["os"], b + 1)
                    wait(act, S["ve3"], b)
                    for t in range(TPB):
                        A(SQS[:, :], OS[:, t, :], ACT.Square, accum_out=SQ[:, t:t + 1]).then_inc(S["sq"], 1)
                        wait(act, S["sq"], 2 * b + t + 1)
                    wait(act, S["osT_ps"], b + 1)
                    wait(act, S["fo_ps"], b)
                    A(OT[:, :, :, :], ps[:, 0, :].rearrange("p (t k n) -> p t k n", t=TPB, k=KT), ACT.Copy)\
                        .then_inc(S["osT"], 1)
                if within(b, 1, B + 1):
                    wait(act, S["fo"], 2 * b)
                    act.dma_start(out[bass.ds((b - 1) * T, T), :].rearrange("(t p) d -> p t d", p=P), FO[:, 1 - u])\
                        .then_inc(S[f"d_out{1 - u}"], 16)

            turns(act, 0, 4, B - 2, B + 1, final)
            act.wait_ge(S["d_out0"], 16 * B // 2)
            act.wait_ge(S["d_out1"], 16 * B // 2)

        @block.vector
        def _(dve):
            V = nc.vector
            V.memset(halves[0:64, 0:1], GN).then_inc(S["halves"], 1)
            V.memset(halves[64:128, 0:1], 0.0).then_inc(S["halves"], 1)
            V.memset(halves[0:64, 1:2], 0.0).then_inc(S["halves"], 1)
            V.memset(halves[64:128, 1:2], GN).then_inc(S["halves"], 1)
            dve.wait_ge(S["csel"], 4)
            V.tensor_scalar(cumT[0:64, :], cumT[0:64, :], GN, None, ALU.subtract).then_inc(S["cumT"], 1)
            dve.wait_ge(S["d_w1"], 16 * 4)
            for k in range(KT):
                V.tensor_scalar(WQG[:, k, :], WQG[:, k, :], vtmp[:, 2, k:k + 1], None, ALU.mult)\
                    .then_inc(S["foldq"], 1)
                V.tensor_scalar(GW[:, k, :], GW[:, k, :], gcol[:, k:k + 1], None, ALU.mult).then_inc(S["foldg"], 1)
            dve.wait_ge(S["m_ps"], 1)
            V.tensor_copy(M2[:, :, :], ps[:, 1, :].rearrange("p (k n) -> p k n", k=KT)).then_inc(S["m2"], 1)
            V.tensor_tensor(CBc[:, :], ps[:, 3, 0:D], bob[:, :], ALU.add).then_inc(S["cb"], 1)
            dve.wait_ge(S["iota"], 6)
            V.tensor_copy(BASE[:, 0, 0, :], eoff[:, :]).then_inc(S["r_b2"], 1)
            dve.wait_ge(S["cb"], 1)
            dve.wait_ge(S["r_b2"], 1)

            def bc(ap, n):
                return ap.unsqueeze(2).broadcast_to([P, ap.shape[1], n])

            def batch(b, u):
                a1, a2, a3 = within(b, -2, B - 2), within(b, -1, B - 1), within(b, 0, B)
                v = 1 - u
                if a2:
                    tl = (b + 1) * TPB
                    wait(dve, S["sump"], b + 2)
                    wait(dve, S["x1"], 2 * b + 2)
                    V.reciprocal(RI[:, :], SUM[:, v, :]).then_inc(S["ri"], 1)
                    wait(dve, S["ri"], b + 2)
                    wait(dve, S["attn_ps"], b + 2)
                    for t in range(TPB):
                        xt = X1[:, bass.ds(tl + t, 1), :].rearrange("p a d -> p (a d)")
                        V.scalar_tensor_tensor(out=xt, in0=ps[:, 2, t * D:(t + 1) * D], scalar=RI[:, t:t + 1],
                                               in1=xt, op0=ALU.mult, op1=ALU.add).then_inc(S["x1"], 1)
                    wait(dve, S["x1"], 2 * b + 4)
                    wait(dve, S["stat2"], b + 1)
                    hold(dve, S["turn_dve"])
                    for t in range(TPB):
                        V.bn_stats(BN2[:, t, :], X1[:, bass.ds(tl + t, 1), :].rearrange("p a d -> p (a d)"))\
                            .then_inc(S["bn2"], 1)
                if a1:
                    wait(dve, S[f"d_x{u}"], 8 * (b + 2 - u) + 16)
                    wait(dve, S["stat1"], b + 2)
                    hold(dve, S["turn_dve"])
                    for t in range(TPB):
                        V.bn_stats(BN1[:, t, :],
                                   X1[:, bass.ds((b + 2) * TPB + t, 1), :].rearrange("p a d -> p (a d)"))\
                            .then_inc(S["bn1"], 1)
                if a2:
                    wait(dve, S["bn2"], 2 * b + 4)
                    wait(dve, S["comb"], b)
                    hold(dve, S["turn_dve"])
                    for t in range(TPB):
                        last = V.bn_aggr(MV2[:, v, t, :], BN2[:, t, :])
                    last.then_inc(S["stat2"], 1)
                if a1:
                    wait(dve, S["bn1"], 2 * b + 6)
                    wait(dve, S["rstd1"], b + 1)
                    hold(dve, S["turn_dve"])
                    for t in range(TPB):
                        last = V.bn_aggr(MV1[:, u, t, :], BN1[:, t, :])
                    last.then_inc(S["stat1"], 1)
                if a3:
                    lg = LG[:, :, :]
                    wait(dve, S["qg_ps"], b + 1)
                    V.tensor_copy(lg, ps[:, 4:6, D:D + E]).then_inc(S["lg"], 1)
                    wait(dve, S["lg"], b + 1)
                    V.tensor_reduce(M1v[:, :], lg, AX, ALU.max).then_inc(S["route"], 1)
                    wait(dve, S["route"], b * 13 + 1)
                    V.tensor_tensor(EQ1[:, :, :], lg, bc(M1v[:, :], E), ALU.is_equal).then_inc(S["route"], 1)
                    wait(dve, S["route"], b * 13 + 2)
                    V.tensor_tensor(EQ1[:, :, :], EQ1[:, :, :], wrev[:, :, :], ALU.mult).then_inc(S["route"], 1)
                    wait(dve, S["route"], b * 13 + 3)
                    V.tensor_reduce(KEY[:, 0, :], EQ1[:, :, :], AX, ALU.max).then_inc(S["route"], 1)
                    wait(dve, S["route"], b * 13 + 4)
                    V.tensor_tensor(SEL[:, 0], wrev[:, :, :], bc(KEY[:, 0, :], E), ALU.is_equal)\
                        .then_inc(S["route"], 1)
                    wait(dve, S["route"], b * 13 + 5)
                    V.scalar_tensor_tensor(out=L2[:, :, :], in0=SEL[:, 0], scalar=-1e30, in1=lg,
                                           op0=ALU.mult, op1=ALU.add).then_inc(S["r_l2"], 1)
                if a2:
                    wait(dve, S["comb"], b + 2)
                    wait(dve, S[f"d_scat{v}"], 32 * (b + 1 - v))
                    for t in range(TPB):
                        last = V.tensor_scalar(ROW[:, v, t, 0:D],
                                               X1[:, bass.ds(tl + t, 1), :].rearrange("p a d -> p (a d)"),
                                               MV2[:, v, t, 0:1], CO2[:, v, t:t + 1], ALU.subtract, ALU.mult)
                    last.then_inc(S["y"], 1)
                if a1:
                    wait(dve, S["rstd1"], b + 3)
                    wait(dve, S["xnT_ps"], b + 2)
                    for t in range(TPB):
                        last = V.tensor_scalar(XN[:, t, :],
                                               X1[:, bass.ds((b + 2) * TPB + t, 1), :].rearrange("p a d -> p (a d)"),
                                               MV1[:, u, t, 0:1], RS1[:, u, t:t + 1], ALU.subtract, ALU.mult)
                    last.then_inc(S["xn"], 1)
                if a3:
                    wait(dve, S["r_l2"], b + 1)
                    V.tensor_reduce(M2v[:, :], L2[:, :, :], AX, ALU.max).then_inc(S["route"], 1)
                    wait(dve, S["route"], b * 13 + 6)
                    V.tensor_tensor(EQ1[:, :, :], L2[:, :, :], bc(M2v[:, :], E), ALU.is_equal)\
                        .then_inc(S["route"], 1)
                    wait(dve, S["route"], b * 13 + 7)
                    V.tensor_tensor(EQ1[:, :, :], EQ1[:, :, :], wrev[:, :, :], ALU.mult).then_inc(S["route"], 1)
                    wait(dve, S["route"], b * 13 + 8)
                    V.tensor_reduce(KEY[:, 1, :], EQ1[:, :, :], AX, ALU.max).then_inc(S["route"], 1)
                    wait(dve, S["route"], b * 13 + 9)
                    V.tensor_tensor(SEL[:, 1], wrev[:, :, :], bc(KEY[:, 1, :], E), ALU.is_equal)\
                        .then_inc(S["route"], 1)
                    wait(dve, S["route"], b * 13 + 10)
                    V.tensor_tensor(MASK[:, :, :], SEL[:, 0], SEL[:, 1], ALU.add).then_inc(S["r_mask"], 1)
                    V.tensor_tensor(D21[:, bass.ds(b * TPB, TPB)], M2v[:, :], M1v[:, :], ALU.subtract)\
                        .then_inc(S["r_meta"], 1)
                    V.tensor_copy(ROW[:, u, :, CB_], bidx[:, bass.ds(b * TPB, TPB)])
                    V.tensor_copy(ROW[:, u, :, CN_], nidx[:, bass.ds(b * TPB, TPB)])
                    V.tensor_scalar(ROW[:, u, :, CE_], KEY[:, 0, :], -1.0, float(E), ALU.mult, ALU.add)\
                        .then_inc(S["r_meta"], 1)
                    wait(dve, S["lq"], b + 1)
                    V.scalar_tensor_tensor(out=AQ[:, :, :], in0=ps[:, 4:6, 0:D], scalar=0.0, in1=LQ[:, :, :],
                                           op0=ALU.min, op1=ALU.subtract).then_inc(S["lsq"], 1)
                if a1:
                    wait(dve, S["kq"], b + 3)
                    wait(dve, S["attn_ps"], b + 1)
                    V.tensor_tensor(VO[:, u, :], ps[0:K, 6, 256:512], CBc[0:K, :], ALU.add).then_inc(S["vo"], 1)
                if a3:
                    wait(dve, S["rank_ps"], b + 1)
                    V.tensor_tensor(BASE[:, u, 1, :], BASE[:, u, 0, :], ps[:, 7, TPB * E:TPB * E + E], ALU.add)\
                        .then_inc(S["route"], 1)
                    wait(dve, S["route"], b * 13 + 11)
                    V.tensor_tensor(BASE[:, v, 0, :], BASE[:, u, 1, :], ps[:, 7, TPB * E + E:TPB * E + 2 * E],
                                    ALU.add).then_inc(S["r_b2"], 1)
                    V.tensor_tensor(POS[:, :, :], ps[:, 7, 0:TPB * E].rearrange("p (t e) -> p t e", t=TPB),
                                    BASE[:, u], ALU.add).then_inc(S["r_pos"], 1)
                    wait(dve, S["r_b2"], b + 2)
                    wait(dve, S["r_pos"], b + 1)
                    V.tensor_tensor(POSK[:, :, :, :], SEL[:, :, :, :],
                                    POS[:, :, :].unsqueeze(1).broadcast_to([P, 2, TPB, E]), ALU.mult)\
                        .then_inc(S["route"], 1)
                    wait(dve, S["route"], b * 13 + 12)
                    V.tensor_reduce(IDF[:, :, :], POSK[:, :, :, :], AX, ALU.add).then_inc(S["route"], 1)
                    wait(dve, S["route"], b * 13 + 13)
                    wait(dve, S[f"d_scat{u}"], 32 * (b - u))
                    V.tensor_copy(IDX[:, u, :], IDF[:, :, :].rearrange("p k t -> p (k t)")).then_inc(S["idx"], 1)
                    wait(dve, S["sgq"], b + 1)
                    V.tensor_tensor(ROW[:, u, :, D:2 * D], ps[:, 4:6, 0:D], EQ[:, :, :], ALU.mult)\
                        .then_inc(S["rowq"], 1)
                if a1:
                    wait(dve, S["s_ps"], b + 3)
                    wait(dve, S["kq"], b + 3)
                    wait(dve, S["sm"], b + 2)
                    V.tensor_tensor(SS[:, :, :], ps[:, 1, 0:TPB * K].rearrange("p (t n) -> p t n", t=TPB),
                                    KQ[:, u, 2, :].unsqueeze(1).broadcast_to([P, TPB, K]), ALU.add)\
                        .then_inc(S["ss"], 1)
                    wait(dve, S["ss"], b + 3)
                    V.tensor_reduce(MX[:, :], SS[:, :, :], AX, ALU.max).then_inc(S["mx"], 1)
                    wait(dve, S["mx"], b + 3)
                    wait(dve, S["p"], b + 2)
                    V.tensor_tensor(SM[:, :, :], SS[:, :, :], bc(MX[:, :], K), ALU.subtract).then_inc(S["sm"], 1)
                    wait(dve, S["p"], b + 3)
                    V.tensor_reduce(SUM[:, u, :], PR[:, :, :], AX, ALU.add).then_inc(S["sump"], 1)

            turns(dve, -2, 4, B - 2, B, batch)

            phase_a_over(dve)
            V.memset(SP_[:, :, :, :, :, :], 0.0).then_inc(S["states0"], 1)
            V.memset(ST[:, :, :, :, :], 0.0).then_inc(S["states0"], 1)

            def step(ins):
                ins.then_inc(S["tab"], 1)
                tab[0] += 1

            def settle():
                dve.wait_ge(S["tab"], tab[0])

            tab = [0]
            step(V.tensor_tensor(PDF[:, :], BASE[:, 0, 0, :], eoff[:, :], ALU.subtract))
            settle()
            step(V.tensor_scalar(CNTI[:, :], PDF[:, :], float(P - 1), None, ALU.add))
            step(V.tensor_copy(PDI[:, :], BASE[:, 0, 0, :]))
            settle()
            step(V.tensor_scalar(NCI[:, :], CNTI[:, :], 7, None, ALU.arith_shift_right))
            settle()
            step(V.tensor_copy(NCF[:, :], NCI[:, :]))
            settle()
            step(V.tensor_scalar(COEF[:, :], NCF[:, :], float(-P), float(REG), ALU.mult, ALU.add))
            step(V.tensor_copy(CEND[:, 0:1], NCF[:, 0:1]))
            settle()
            for e in range(1, E):
                step(V.tensor_tensor(CEND[:, e:e + 1], CEND[:, e - 1:e], NCF[:, e:e + 1], ALU.add))
                settle()
            step(V.tensor_scalar(RTAB[:, :], cio[:, :], float(P), None, ALU.mult))
            for e in range(E):
                step(V.tensor_scalar(GE[:, e, :], cio[:, :], CEND[:, e:e + 1], None, ALU.is_ge))
            settle()
            step(V.tensor_copy(ECOL[:, :], GE[:, 0, :]))
            settle()
            for e in range(E):
                if e:
                    step(V.tensor_tensor(ECOL[:, :], ECOL[:, :], GE[:, e, :], ALU.add))
                step(V.scalar_tensor_tensor(out=RTAB[:, :], in0=GE[:, e, :], scalar=COEF[:, e:e + 1],
                                            in1=RTAB[:, :], op0=ALU.mult, op1=ALU.add))
                settle()
            step(V.tensor_copy(RTI[:, :], RTAB[:, :]))
            step(V.tensor_scalar(ECOLB[:, :], ECOL[:, :], float(B), None, ALU.mult))
            step(V.tensor_scalar(ETI[:, :], ECOL[:, :], float(E - 1), None, ALU.min))
            settle()
            dve.wait_ge(S["d_W"], 16)
            for k in range(KT):
                V.tensor_scalar(W[:, :, k * 3 * D:(k + 1) * 3 * D], W[:, :, k * 3 * D:(k + 1) * 3 * D],
                                vtmp[:, 2, k:k + 1], None, ALU.mult).then_inc(S["foldw"], 1)
            dve.wait_ge(S["states0"], 2)
            V.memset(SEGL[:, 1, :], -1.0).then_inc(S["segl"], 1)
            V.memset(EF[:, 1, :, :], 0.0).then_inc(S["ef"], 1)
            V.memset(CONT[:, :, :], 0.0).then_inc(S["tables"], 1)
            dve.wait_ge(S["segl"], 1)
            dve.wait_ge(S["ef"], 1)

            def chunk(c, u):
                n, v = c + 1, 1 - u
                s1, s2 = within(c, -1, NCH - 1), within(c, 0, NCH)
                if s2:
                    wait(dve, S["ok_ps"], c + 1)
                    wait(dve, S["dec"], c + 1)
                    V.tensor_tensor(OKD[:, :], ps[:, 4, 256:512], DEC[:, u], ALU.mult).then_inc(S["okd"], 1)
                    wait(dve, S["okd"], c + 1)
                    V.tensor_reduce(MXO[:, :], OKD[:, :].rearrange("p (h m) -> p h m", h=HEADS), AX, ALU.max)\
                        .then_inc(S["mxo"], 1)
                    wait(dve, S["mxo"], c + 1)
                    wait(dve, S["eo"], c)
                    V.tensor_tensor(SBO[:, :].rearrange("p (h m) -> p h m", h=HEADS),
                                    OKD[:, :].rearrange("p (h m) -> p h m", h=HEADS), bc(MXO[:, :], HD),
                                    ALU.subtract).then_inc(S["sbo"], 1)
                    wait(dve, S["eo"], c + 1)
                    wait(dve, S["qvgT_ps"], c)
                    V.tensor_tensor(QVG[:, :], EO[:, :], DEC[:, u], ALU.mult).then_inc(S["qvg"], 1)
                if s1:
                    wait(dve, S["seg_ps"], n + 1)
                    sg = ps[:, 3, 0:P]
                    wait(dve, S["cont"], n)
                    wait(dve, S["sla"], n - 1)
                    V.tensor_copy(SEGL[:, v, :], sg[:, P - 1:P]).then_inc(S["segl"], 1)
                    V.scalar_tensor_tensor(out=MSK[:, v], in0=sg, scalar=META[:, v, 0:1], in1=triM[:, :],
                                           op0=ALU.is_equal, op1=ALU.mult).then_inc(S["msk"], 1)
                    wait(dve, S["qvm"], n - 1)
                    wait(dve, S["qtm"], n - 1)
                    V.tensor_scalar(RM[:, v], sg, SEGL[:, u, :], None, ALU.is_equal).then_inc(S["rm"], 1)
                if s2:
                    V.tensor_reduce(SMO[:, :], EO[:, :].rearrange("p (h m) -> p h m", h=HEADS), AX, ALU.add)\
                        .then_inc(S["smo"], 1)
                    wait(dve, S["qvgT_ps"], c + 1)
                    wait(dve, S["t_ps"], c)
                    wait(dve, S["qvm"], c)
                    V.tensor_copy(QVGT[:, :, :], ps[:, 3, 256:512].rearrange("p (a n) -> p a n", a=2))\
                        .then_inc(S["qvgT"], 1)
                    wait(dve, S["smo"], c + 1)
                    V.reciprocal(RIN[:, u, :], SMO[:, :]).then_inc(S["rin"], 1)
                if s1:
                    wait(dve, S["ln"], n + 1)
                    wait(dve, S["f_ps"], n - 1)
                    wait(dve, S["eg"], n - 1)
                    V.scalar_tensor_tensor(out=LS[:, v, :], in0=ps[:, 0, :], scalar=0.0, in1=LN_[:, :],
                                           op0=ALU.min, op1=ALU.subtract).then_inc(S["ls"], 1)
                if s2:
                    wait(dve, S["t_ps"], c + 1)
                    wait(dve, S["msk"], c + 1)
                    wait(dve, S["ov_ps"], c)
                    V.tensor_tensor(TM[:, :, :].rearrange("p (a b) n -> p b a n", b=2),
                                    ps[:, 4:6, 0:256].rearrange("p b (a n) -> p b a n", a=2),
                                    MSK[:, u].unsqueeze(1).unsqueeze(1).broadcast_to([P, 2, 2, P]), ALU.mult)\
                        .then_inc(S["tm"], 1)
                if s1:
                    wait(dve, S["sg"], n + 1)
                    wait(dve, S["h_ps"], n - 1)
                    V.tensor_tensor(KV[:, v, 0, :, :], ps[:, 0, D:2 * D].rearrange("p (h d) -> p h d", h=HEADS),
                                    SG[:, :].rearrange("p (h d) -> p h d", h=HEADS), ALU.mult).then_inc(S["kk"], 1)
                    wait(dve, S["en"], n + 1)
                    wait(dve, S["eg"], n + 1)
                    wait(dve, S["ok_ps"], n - 1)
                    V.scalar_tensor_tensor(out=SIN[:, v], in0=EG[:, :], scalar=1.0, in1=EN[:, :],
                                           op0=ALU.subtract, op1=ALU.mult, reverse0=True).then_inc(S["sin"], 1)
                if s2:
                    wait(dve, S["ov_ps"], c + 1)
                    wait(dve, S["rin"], c + 1)
                    wait(dve, S[f"d_o{u}"], 8 * (c - u))
                    V.tensor_tensor(OV[:, u].rearrange("p (h d) -> p h d", h=HEADS),
                                    ps[:, 5, 256:512].rearrange("p (h d) -> p h d", h=HEADS),
                                    bc(RIN[:, u, :], HD), ALU.mult).then_inc(S["ov"], 1)
                if s1:
                    wait(dve, S["a_ps"], n + 1)
                    V.tensor_tensor(AM[:, v].rearrange("p (a b) n -> p b a n", b=2),
                                    ps[:, 4:6, 0:256].rearrange("p b (a n) -> p b a n", a=2),
                                    MSK[:, v].unsqueeze(1).unsqueeze(1).broadcast_to([P, 2, 2, P]), ALU.mult)\
                        .then_inc(S["am"], 1)
                    wait(dve, S["h_ps"], n + 1)
                    wait(dve, S["sp"], n + 1)
                    wait(dve, S["cont"], n + 1)
                    for h in range(2):
                        q = slice(HD * h, HD * h + HD)
                        V.scalar_tensor_tensor(
                            out=ST[q, :, :, h, :].rearrange("p a k d -> p (a k) d"),
                            in0=SP_[q, v, :, :, h, :].rearrange("p a k d -> p (a k) d"), scalar=CONT[q, v, :],
                            in1=ps[q, 7, 0:256].rearrange("p (a d) -> p a d", a=4),
                            op0=ALU.mult, op1=ALU.add).then_inc(S["st"], 1)

            turns(dve, -1, 4, NCH - 2, NCH, chunk)

            dve.wait_ge(S["rwe"], 1)
            V.tensor_scalar(RW1[:, :], RWT[:, :], 1.0, None, ALU.add).then_inc(S["rwd"], 1)
            dve.wait_ge(S["rwd"], 1)
            V.reciprocal(RW1[:, :], RW1[:, :]).then_inc(S["rw"], 1)
            dve.wait_ge(S["rw"], 1)
            V.tensor_tensor(RW2[:, :], RWT[:, :], RW1[:, :], ALU.mult).then_inc(S["rw"], 1)
            dve.wait_ge(S["rw"], 2)

            def final(b, u):
                v = 1 - u
                if within(b, 0, B):
                    wait(dve, S[f"d_oc{u}"], 16 * (b - u) + 32)
                    wait(dve, S["os"], b)
                    for t in range(TPB):
                        last = V.tensor_scalar(OM[:, t, :], OC[:, u, 1, t, :], RW2[:, bass.ds(b * TPB + t, 1)],
                                               None, ALU.mult)
                    last.then_inc(S["om"], 1)
                    wait(dve, S["om"], b + 1)
                    wait(dve, S["osT_ps"], b)
                    wait(dve, S["sq"], 2 * b)
                    for t in range(TPB):
                        last = V.scalar_tensor_tensor(out=OS[:, t, :], in0=OC[:, u, 0, t, :],
                                                      scalar=RW1[:, bass.ds(b * TPB + t, 1)], in1=OM[:, t, :],
                                                      op0=ALU.mult, op1=ALU.add)
                    last.then_inc(S["os"], 1)
                if within(b, 1, B + 1):
                    wait(dve, S["fo_ps"], b)
                    wait(dve, S["rs3"], b)
                    wait(dve, S[f"d_out{v}"], 8 * (b - 1 - v))
                    for t in range(TPB):
                        V.scalar_tensor_tensor(
                            out=FO[:, v, t, :], in0=ps[:, 1 + v, t * D:(t + 1) * D], scalar=RS3[:, v, t:t + 1],
                            in1=X1[:, bass.ds((b - 1) * TPB + t, 1), :].rearrange("p a d -> p (a d)"),
                            op0=ALU.mult, op1=ALU.add).then_inc(S["fo"], 1)

            turns(dve, 0, 4, B - 2, B + 1, final)


_INS = ['x', 'ctxT', 'wk', 'wq', 'wv', 'woT', 'bqc', 'bvc', 'bo', 'nwc', 'wqgT', 'wfkvT', 'gwc', 'fwoT']


def kernel(x, ctx_1024, L0_xattn_Wk, L0_xattn_Wv, L0_xattn_bv, L0_xattn_Wq, L0_xattn_bq, L0_xattn_Wo, L0_xattn_bo,
           L0_ffn_norm_w, L0_ffn_Wg, L0_ffn_Wq, L0_ffn_Wk, L0_ffn_Wv, L0_ffn_Wf, L0_ffn_gnorm_w, L0_ffn_Wo):
    import numpy as np
    import concourse.bacc as bacc
    from concourse.bass_utils import run_bass_kernel_spmd

    def col(v):
        return np.asarray(v).reshape(KT, P).T

    fkv = np.concatenate([np.asarray(L0_ffn_Wf), np.asarray(L0_ffn_Wk), np.asarray(L0_ffn_Wv)], axis=1)
    fkv = fkv.transpose(2, 0, 1).reshape(KT, P, E, 3 * D).transpose(1, 2, 0, 3).reshape(P, E, KT * 3 * D)
    data = {
        'x': np.asarray(x).reshape(B * T, D),
        'ctxT': np.asarray(ctx_1024).transpose(0, 2, 1).reshape(B * D, K),
        'wk': L0_xattn_Wk, 'wq': L0_xattn_Wq, 'wv': L0_xattn_Wv, 'woT': np.asarray(L0_xattn_Wo).T,
        'bqc': col(L0_xattn_bq), 'bvc': col(L0_xattn_bv), 'bo': L0_xattn_bo, 'nwc': col(L0_ffn_norm_w),
        'wqgT': np.concatenate([np.asarray(L0_ffn_Wq), np.asarray(L0_ffn_Wg)], axis=0).T,
        'wfkvT': fkv, 'gwc': col(L0_ffn_gnorm_w), 'fwoT': np.asarray(L0_ffn_Wo).T,
    }
    nc = bacc.Bacc("TRN2", target_bir_lowering=False, num_devices=1)
    arrays, args = {}, []
    for name in _INS:
        a = np.ascontiguousarray(data[name])
        arrays[f"in_{name}"] = a
        args.append(nc.dram_tensor(f"in_{name}", a.shape, mybir.dt.from_np(a.dtype), kind="ExternalInput").ap())
    args.append(nc.dram_tensor("out_0", (B * T, D), F32, kind="ExternalOutput").ap())
    xattn_gsa_moe(nc, *args)
    r = run_bass_kernel_spmd(nc, [arrays], core_ids=[0])
    return r.results[0]["out_0"].reshape(B, T, D)
```

```python
from contextlib import ExitStack

import concourse.bass as bass
from concourse import mybir

ALU = mybir.AluOpType
ACT = mybir.ActivationFunctionType
F32 = mybir.dt.float32
I32 = mybir.dt.int32
AX = mybir.AxisListType.X

P = 128
B, T, D = 32, 256, 256
K = 77
E, HEADS, HD = 8, 4, 64
TPB = T // P
KT = D // P
NT = B * T // P
EPS = 1e-5
ISQ = D ** -0.5
GN = 1.0 / 8.0

REG = B * T + P
NCH = 2 * B * T // P + E
PADROW = E * REG
WPC = KT * E * 3 * D // B
RW = 2 * D + 4
CB_, CN_, CE_, CU_ = 2 * D, 2 * D + 1, 2 * D + 2, 2 * D + 3
NOUT = 3 * B * T + P


def wait(eng, sem, count):
    if isinstance(count, int) and count <= 0:
        return
    eng.wait_ge(sem, count)


def turns(eng, first, lo, hi, last, body):
    for b in range(first, lo):
        body(b, b % 2)
    with eng.Fori(lo // 2, hi // 2) as i:
        for u in range(2):
            body(i * 2 + u, u)
    for b in range(hi, last):
        body(b, b % 2)


def hold(eng, sem):
    eng.sem_inc(sem, 1)


def within(b, lo, hi):
    return not isinstance(b, int) or lo <= b < hi


def xattn_gsa_moe(nc, x, ctxT, wk, wq, wv, woT, bqc, bvc, bo, nwc, wqgT, wfkvT, gwc, fwoT, out):
    with ExitStack() as ctx:
        def sb(name, shape, dt=F32):
            return ctx.enter_context(nc.sbuf_tensor(name, shape, dt))

        S = {}

        def sem(*names):
            for n in names:
                S[n] = ctx.enter_context(nc.semaphore(n))

        rows_d = nc.dram_tensor("rows_d", [PADROW + E * P, RW], F32).ap()
        exp_d = nc.dram_tensor("exp_d", [NOUT, D], F32).ap()

        ps = ctx.enter_context(nc.psum_tensor("ps", [P, 8, 512], F32))

        X1 = sb("X1", [P, NT, D])
        W = sb("W", [P, KT, E * 3 * D])
        GW = sb("GW", [P, KT, D])
        ident = sb("ident", [P, P])
        triM = sb("triM", [P, P])
        triS = sb("triS", [P, P])
        cumT = sb("cumT", [P, P])
        halves = sb("halves", [P, 2])
        ones = sb("ones", [P, P])
        mhalf = sb("mhalf", [P, 2])
        nidx = sb("nidx", [P, NT])
        bidx = sb("bidx", [P, NT])
        D21 = sb("D21", [P, NT])
        RW1 = sb("RW1", [P, NT])
        RW2 = sb("RW2", [P, NT])
        RWT = sb("RWT", [P, NT])
        vtmp = sb("vtmp", [P, 3, KT])
        gcol = sb("gcol", [P, KT])
        PADR = sb("PADR", [P, RW])
        BASE = sb("BASE", [P, 2, TPB, E])
        eoff = sb("eoff", [P, E])
        cio = sb("cio", [P, NCH])
        CNTI = sb("CNTI", [P, E], I32)
        NCI = sb("NCI", [P, E], I32)
        NCF = sb("NCF", [P, E])
        CEND = sb("CEND", [P, E])
        COEF = sb("COEF", [P, E])
        GE = sb("GE", [P, E, NCH])
        ECOL = sb("ECOL", [P, NCH])
        ECOLB = sb("ECOLB", [P, NCH])
        RTAB = sb("RTAB", [P, NCH])
        ETI = sb("ETI", [P, NCH], I32)
        RTI = sb("RTI", [P, NCH], I32)
        PDF = sb("PDF", [P, E])
        PDI = sb("PDI", [P, E], I32)
        keep, phase = ctx, ExitStack()
        ctx = phase
        wtmp = sb("wtmp", [P, 4, KT, D])
        M1 = sb("M1", [P, KT, D])
        M2 = sb("M2", [P, KT, D])
        wb = sb("wb", [P, KT])
        CBc = sb("CBc", [P, D])
        bob = sb("bob", [P, D])
        WQG = sb("WQG", [P, KT, D + E])
        wrev = sb("wrev", [P, TPB, E])
        CTX = sb("CTX", [P, 2, KT, K])
        KQ = sb("KQ", [P, 2, 3, K])
        VO = sb("VO", [K, 2, D])
        BN1 = sb("BN1", [P, TPB, 6])
        MV1 = sb("MV1", [P, 2, TPB, 2])
        VE1 = sb("VE1", [P, 2, TPB])
        RS1 = sb("RS1", [P, 2, TPB])
        XN = sb("XN", [P, TPB, D])
        XNT = sb("XNT", [P, TPB, KT, P])
        SS = sb("SS", [P, TPB, K])
        MX = sb("MX", [P, TPB])
        SM = sb("SM", [P, TPB, K])
        PR = sb("PR", [P, TPB, K])
        SUM = sb("SUM", [P, 2, TPB])
        RI = sb("RI", [P, TPB])
        PT = sb("PT", [K, 2, TPB, P])
        BN2 = sb("BN2", [P, TPB, 6])
        MV2 = sb("MV2", [P, 2, TPB, 2])
        VE2 = sb("VE2", [P, 2, TPB])
        CO2 = sb("CO2", [P, 2, TPB])
        NM1 = sb("NM1", [P, 2, TPB])
        NM2 = sb("NM2", [P, 2, TPB])
        MB1 = sb("MB1", [P, 2, TPB])
        MB2 = sb("MB2", [P, 2, TPB])
        ROW = sb("ROW", [P, 2, TPB, RW])
        YB = sb("YB", [P, TPB, D])
        YT = sb("YT", [P, TPB, KT, P])
        AQ = sb("AQ", [P, TPB, D])
        EQ = sb("EQ", [P, TPB, D])
        LQ = sb("LQ", [P, TPB, D])
        M1v = sb("M1v", [P, TPB])
        M2v = sb("M2v", [P, TPB])
        EQ1 = sb("EQ1", [P, TPB, E])
        KEY = sb("KEY", [P, 2, TPB])
        SEL = sb("SEL", [P, 2, TPB, E])
        L2 = sb("L2", [P, TPB, E])
        LG = sb("LG", [P, TPB, E])
        MASK = sb("MASK", [P, TPB, E])
        POS = sb("POS", [P, TPB, E])
        POSK = sb("POSK", [P, 2, TPB, E])
        IDF = sb("IDF", [P, 2, TPB])
        IDX = sb("IDX", [P, 2, 2 * TPB], I32)
        phase.close()
        ctx = keep
        X = sb("X", [P, 2, RW])
        META = sb("META", [P, 2, 4])
        IDO = sb("IDO", [P, 2, 1], I32)
        XT = sb("XT", [P, 2, 4, P])
        AB = sb("AB", [P, 2 * D])
        LN_ = sb("LN_", [P, 2 * D])
        LS = sb("LS", [P, 2, 2 * D])
        SG = sb("SG", [P, D])
        EG = sb("EG", [P, D])
        KV = sb("KV", [P, 2, 2, HEADS, HD])
        DEC = sb("DEC", [P, 2, D])
        EN = sb("EN", [P, D])
        EF = sb("EF", [P, 2, 2, 2])
        SIN = sb("SIN", [P, 2, D])
        SLA = sb("SLA", [P, 2, D])
        KST = sb("KST", [P, 2, 4, P])
        MSK = sb("MSK", [P, 2, P])
        RM = sb("RM", [P, 2, P])
        SEGL = sb("SEGL", [P, 2, 1])
        CONT = sb("CONT", [P, 2, 1])
        FAC = sb("FAC", [P, 2, 2])
        AM = sb("AM", [P, 2, HEADS, P])
        QTM = sb("QTM", [P, 2, 2, P])
        SP_ = sb("SP_", [P, 2, 2, 2, 2, HD])
        ST = sb("ST", [P, 2, 2, 2, HD])
        HK = sb("HK", [P, 2, 2, P])
        OKD = sb("OKD", [P, D])
        MXO = sb("MXO", [P, HEADS])
        SBO = sb("SBO", [P, D])
        EO = sb("EO", [P, D])
        SMO = sb("SMO", [P, HEADS])
        RIN = sb("RIN", [P, 2, HEADS])
        QVG = sb("QVG", [P, D])
        QVGT = sb("QVGT", [P, 2, P])
        QVM = sb("QVM", [P, 2, P])
        TM = sb("TM", [P, HEADS, P])
        OV = sb("OV", [P, 2, D])
        OC = sb("OC", [P, 2, 2, TPB, D])
        OS = sb("OS", [P, TPB, D])
        OM = sb("OM", [P, TPB, D])
        SQ = sb("SQ", [P, TPB])
        SQS = sb("SQS", [P, D])
        VE3 = sb("VE3", [P, TPB])
        RS3 = sb("RS3", [P, 2, TPB])
        OT = sb("OT", [P, TPB, KT, P])
        FO = sb("FO", [P, 2, TPB, D])

        sem("d_w0", "d_w1", "d_W", "d_x0", "d_x1", "d_c0", "d_c1", "d_pad", "d_scat0", "d_scat1", "d_padw",
            "d_row0", "d_row1", "d_o0", "d_o1", "d_oc0", "d_oc1", "d_out0", "d_out1")
        sem("iota", "cmem", "csel", "cumT", "halves", "foldq", "foldw", "foldg", "m_ps", "m1", "m2", "wb", "cb")
        sem("bn1", "stat1", "ve1", "rstd1", "xn", "xnT_ps", "xnT", "kq_ps", "kq", "vo", "s_ps", "ss", "mx", "sm",
            "p", "sump", "pT_ps", "pT", "attn_ps", "ri", "x1", "bn2", "stat2", "ve2", "comb", "y", "yT_ps", "yT",
            "qg_ps", "aq", "eq", "lq", "lsq", "sgq", "rowq", "route", "r_l2", "lg",
            "r_mask", "r_meta", "rank_ps", "r_b2", "r_pos",
            "idx", "turn_pool", "turn_dve", "turn_act")
        sem("tab", "tables", "zero", "states0")
        sem("xT_ps", "xT", "fk_ps", "seg_ps", "v_ps", "ab", "ex", "ln", "ls", "sg", "eg", "kk", "vv", "g_ps", "f_ps",
            "dec", "en", "ef", "sin", "seg", "last", "sla", "kT_ps", "kT", "msk", "rm", "segl",
            "cont", "fac", "a_ps", "am", "qtm", "h_ps", "sp", "st", "hk_ps", "hk", "ok_ps", "okd", "mxo", "sbo",
            "eo", "smo", "rin", "qvg", "qvgT_ps", "qvgT", "qvm", "t_ps", "tm", "ov_ps", "ov", "ido")
        sem("seg2", "seg3", "rwd", "rwe", "rw", "om", "os", "sq", "ve3", "rs3", "osT_ps", "osT", "fo_ps", "fo")

        block = ctx.enter_context(nc.Block())

        def phase_a_over(eng):
            for name, per in (("attn_ps", 1), ("x1", 2), ("ri", 1), ("y", 2), ("yT", 1), ("qg_ps", 1), ("s_ps", 1), ("pT_ps", 1),
                              ("pT", 1), ("sump", 1), ("kq", 1), ("vo", 1), ("comb", 2), ("rstd1", 2), ("rowq", 1),
                              ("sgq", 1), ("idx", 1), ("xn", 1), ("xnT", 1), ("rank_ps", 1)):
                eng.wait_ge(S[name], per * B)
            for u in range(2):
                eng.wait_ge(S[f"d_scat{u}"], 64 * B // 2)

        @block.sync
        def _(sp):
            for i, w_ in enumerate((wk, wq, wv, woT)):
                sp.dma_start(wtmp[:, i], w_.rearrange("(k p) n -> p k n", p=P)).then_inc(S["d_w0"], 16)
            sp.dma_start(vtmp[:, 0], bqc).then_inc(S["d_w0"], 16)
            sp.dma_start(vtmp[:, 1], bvc).then_inc(S["d_w0"], 16)
            sp.dma_start(bob[:, :], bo.partition_broadcast(P)).then_inc(S["d_w0"], 16)
            sp.dma_start(vtmp[:, 2], nwc).then_inc(S["d_w1"], 16)
            sp.dma_start(gcol[:, :], gwc).then_inc(S["d_w1"], 16)
            sp.dma_start(WQG[:, :, :], wqgT.rearrange("(k p) n -> p k n", p=P)).then_inc(S["d_w1"], 16)
            sp.dma_start(GW[:, :, :], fwoT.rearrange("(k p) n -> p k n", p=P)).then_inc(S["d_w1"], 16)
            before, ready = sp.alloc_register("before"), sp.alloc_register("ready")

            def load(b, u):
                if isinstance(b, int):
                    nb, nr = b - 1, 8 * (b - u)
                else:
                    sp.reg_add(before, b, -1)
                    sp.reg_mul(ready, b - u, 8)
                    nb, nr = before, ready
                wait(sp, S["kq_ps"], nb)
                wait(sp, S["d_x0" if u == 0 else "d_x1"], nr)
                sp.dma_start(X1[:, bass.ds(b * TPB, TPB), :],
                             x[bass.ds(b * T, T), :].rearrange("(t p) d -> p t d", p=P)).then_inc(S[f"d_x{u}"], 16)
                sp.dma_start(CTX[:, u], ctxT[bass.ds(b * D, D), :].rearrange("(k p) n -> p k n", p=P))\
                    .then_inc(S[f"d_c{u}"], 16)

            turns(sp, 0, 4, B - 2, B, load)
            sp.wait_ge(S["zero"], 3)
            for i in range(E):
                sp.dma_start(rows_d[PADROW + i * P:PADROW + (i + 1) * P, :], PADR[:, :]).then_inc(S["d_pad"], 16)
            sp.wait_ge(S["tables"], 1)
            for e in range(E):
                r = sp.value_load(PDI[0:1, e:e + 1], min_val=0, max_val=PADROW)
                sp.dma_start(rows_d[bass.ds(r, P), :], PADR[:, :]).then_inc(S["d_padw"], 16)
            sp.wait_ge(S["d_pad"], 16 * E)
            sp.wait_ge(S["d_padw"], 16 * E)
            phase_a_over(sp)
            used = sp.alloc_register("used")

            def row(c, u):
                if isinstance(c, int):
                    nu = c - 1
                else:
                    sp.reg_add(used, c, -1)
                    nu = used
                r = sp.value_load(RTI[0:1, bass.ds(c, 1)], min_val=0, max_val=PADROW + (E - 1) * P)
                wait(sp, S["seg_ps"], nu)
                wait(sp, S["msk"], nu)
                wait(sp, S["ido"], nu)
                wait(sp, S["xT_ps"], nu)
                sp.dma_start(X[:, u, :], rows_d[bass.ds(r, P), :]).then_inc(S[f"d_row{u}"], 16)

            turns(sp, 0, 4, NCH - 2, NCH, row)
            sp.wait_ge(S["d_o0"], 16 * NCH // 2)
            sp.wait_ge(S["d_o1"], 16 * NCH // 2)

            def pair(b, u):
                if isinstance(b, int):
                    nu = b - 1
                else:
                    sp.reg_add(used, b, -1)
                    nu = used
                wait(sp, S["os"], nu)
                for k in range(2):
                    sp.dma_start(OC[:, u, k], exp_d[bass.ds(b * T + k * B * T, T), :]
                                 .rearrange("(t p) d -> p t d", p=P)).then_inc(S[f"d_oc{u}"], 16)

            turns(sp, 0, 4, B - 2, B, pair)

        @block.gpsimd
        def _(g):
            i_ = lambda t, pat, base, cm: nc.gpsimd.iota(t, pat, base=base, channel_multiplier=cm,
                                                         allow_small_or_imprecise_dtypes=True).then_inc(S["iota"], 1)
            g.memset(ident[:, :], 0.0).then_inc(S["cmem"], 1)
            g.memset(triM[:, :], 1.0).then_inc(S["cmem"], 1)
            g.memset(triS[:, :], 1.0).then_inc(S["cmem"], 1)
            g.memset(cumT[:, :], GN).then_inc(S["cmem"], 1)
            g.memset(ones[:, :], 1.0).then_inc(S["cmem"], 1)
            g.memset(mhalf[:, :], -0.5).then_inc(S["cmem"], 1)
            g.wait_ge(S["cmem"], 6)
            sel = lambda t, op, cm, st, fill: g.affine_select(
                out=t, in_=t, compare_op=op, fill=fill, base=0, pattern=[[st, P]], channel_multiplier=cm)\
                .then_inc(S["csel"], 1)
            sel(ident[:, :], ALU.not_equal, 1, -1, 1.0)
            i_(wrev[:, :, :], [[0, TPB], [-1, E]], E, 0)
            i_(eoff[:, :], [[REG, E]], 0, 0)
            i_(nidx[:, :], [[P, NT]], B * T, 1)
            i_(bidx[:, :], [[1, B], [0, TPB]], 0, 0)
            i_(cio[:, :], [[1, NCH]], 0, 0)
            sel(triM[:, :], ALU.is_ge, -1, 1, 0.0)
            sel(triS[:, :], ALU.is_gt, -1, 1, 0.0)
            sel(cumT[:, :], ALU.is_ge, -1, 1, 0.0)
            g.memset(PADR[:, :], 0.0).then_inc(S["zero"], 1)
            g.wait_ge(S["zero"], 1)
            g.memset(PADR[:, CB_:CB_ + 1], -0.5).then_inc(S["zero"], 1)
            i_(PADR[:, CN_:CN_ + 1], [[0, 1]], 3 * B * T, 1)
            g.memset(ROW[:, :, :, CU_:CU_ + 1], 0.0).then_inc(S["cmem"], 1)
            g.wait_ge(S["iota"], 6)
            g.wait_ge(S["zero"], 2)
            g.wait_ge(S["cmem"], 7)
            g.memset(PADR[:, CU_:CU_ + 1], 0.0).then_inc(S["zero"], 1)

            def batch(b, u):
                v = 1 - u
                if within(b, -3, B - 3):
                    m = b + 3
                    wait(g, S["stat1"], m + 1)
                    wait(g, S["xn"], m - 1)
                    hold(g, S["turn_pool"])
                    g.tensor_scalar(VE1[:, v, :], MV1[:, v, :, 1], 1.0, EPS, ALU.mult, ALU.add)\
                        .then_inc(S["ve1"], 1)
                    g.tensor_scalar(NM1[:, v, :], MV1[:, v, :, 0], -1.0, 0.0, ALU.mult, ALU.add)\
                        .then_inc(S["ve1"], 1)
                    wait(g, S["ve1"], 2 * m + 2)
                    g.tensor_tensor(RS1[:, v, :], VE1[:, v, :], mhalf[:, :], ALU.pow).then_inc(S["rstd1"], 1)
                    wait(g, S["rstd1"], 2 * m + 1)
                    g.tensor_tensor(MB1[:, v, :], NM1[:, v, :], RS1[:, v, :], ALU.mult).then_inc(S["rstd1"], 1)
                if within(b, -1, B - 1):
                    m = b + 1
                    wait(g, S["stat2"], m + 1)
                    wait(g, S["y"], 2 * m - 2)
                    hold(g, S["turn_pool"])
                    g.tensor_scalar(VE2[:, v, :], MV2[:, v, :, 1], 1.0 + EPS, EPS * EPS, ALU.mult, ALU.add)\
                        .then_inc(S["ve2"], 1)
                    g.tensor_scalar(NM2[:, v, :], MV2[:, v, :, 0], -1.0, 0.0, ALU.mult, ALU.add)\
                        .then_inc(S["ve2"], 1)
                    wait(g, S["ve2"], 2 * m + 2)
                    g.tensor_tensor(CO2[:, v, :], VE2[:, v, :], mhalf[:, :], ALU.pow).then_inc(S["comb"], 1)
                    wait(g, S["comb"], 2 * m + 1)
                    g.tensor_tensor(MB2[:, v, :], NM2[:, v, :], CO2[:, v, :], ALU.mult).then_inc(S["comb"], 1)
                if within(b, 1, B + 1):
                    m = b - 1
                    wait(g, S["idx"], m + 1)
                    wait(g, S["rowq"], m + 1)
                    wait(g, S["y"], 2 * m + 2)
                    wait(g, S["r_meta"], 2 * m + 2)
                    hold(g, S["turn_pool"])
                    for k in range(2):
                        for t in range(TPB):
                            g.indirect_dma_start(rows_d, bass.IndirectOffsetOnAxis(
                                ap=IDX[:, v, k * TPB + t:k * TPB + t + 1], axis=0), ROW[:, v, t, :], None)\
                                .then_inc(S[f"d_scat{v}"], 16)

            turns(g, -3, 4, B - 4, B + 1, batch)

            def chunk(c, u):
                n, v = c + 1, 1 - u
                s1, s2 = within(c, -1, NCH - 1), within(c, 0, NCH)
                if s1:
                    wait(g, S[f"d_row{v}"], 8 * (n - v) + 16)
                    wait(g, S["msk"], n - 1)
                    hold(g, S["turn_pool"])
                    g.tensor_tensor(META[:, v, 0:1], ECOLB[:, bass.ds(n, 1)], X[:, v, CB_:CB_ + 1], ALU.add)\
                        .then_inc(S["seg"], 1)
                    g.tensor_tensor(META[:, v, 1:2], ECOL[:, bass.ds(n, 1)], X[:, v, CE_:CE_ + 1], ALU.subtract)\
                        .then_inc(S["seg2"], 1)
                    wait(g, S["seg2"], n + 1)
                    hold(g, S["turn_pool"])
                    g.tensor_scalar(META[:, v, 2:3], META[:, v, 1:2], 0.0, -float(B * T), ALU.is_equal, ALU.mult)\
                        .then_inc(S["seg3"], 1)
                    wait(g, S["seg3"], 2 * n + 1)
                    g.tensor_tensor(META[:, v, 1:2], META[:, v, 2:3], X[:, v, CN_:CN_ + 1], ALU.add)\
                        .then_inc(S["seg3"], 1)
                    wait(g, S["seg3"], 2 * n + 2)
                    wait(g, S[f"d_o{v}"], 8 * (n - v))
                    hold(g, S["turn_pool"])
                    g.tensor_copy(IDO[:, v, :], META[:, v, 1:2])\
                        .then_inc(S["ido"], 1)
                    wait(g, S["segl"], n + 2)
                    wait(g, S["st"], 2 * n - 2)
                    hold(g, S["turn_pool"])
                    g.tensor_scalar(META[:, v, 3:4], META[:, v, 0:1], SEGL[:, v, :], 1.0, ALU.is_equal, ALU.mult)\
                        .then_inc(S["last"], 1)
                    g.tensor_scalar(CONT[:, v, :], SEGL[:, u, :], SEGL[:, v, :], 1.0, ALU.is_equal, ALU.mult)\
                        .then_inc(S["cont"], 1)
                    wait(g, S["rm"], n + 1)
                    wait(g, S["xT"], n + 1)
                    wait(g, S["ok_ps"], n - 1)
                    g.tensor_tensor(QTM[:, v], XT[:, v, 2:4, :],
                                    RM[:, v].unsqueeze(1).broadcast_to([P, 2, P]), ALU.mult).then_inc(S["qtm"], 1)
                if s2:
                    wait(g, S["qvgT"], c + 1)
                    wait(g, S["ov_ps"], c)
                    g.tensor_tensor(QVM[:, :, :], QVGT[:, :, :],
                                    RM[:, u].unsqueeze(1).broadcast_to([P, 2, P]), ALU.mult).then_inc(S["qvm"], 1)
                if s1:
                    wait(g, S["ef"], n + 2)
                    wait(g, S["sp"], n - 1)
                    g.tensor_tensor(FAC[:, v, :], EF[:, u, :, 1], EF[:, v, :, 0], ALU.mult).then_inc(S["fac"], 1)
                    wait(g, S["sin"], n + 1)
                    wait(g, S["last"], n + 1)
                    wait(g, S["h_ps"], n - 1)
                    hold(g, S["turn_pool"])
                    g.tensor_scalar(SLA[:, v], SIN[:, v], META[:, v, 3:4], 1.0, ALU.mult, ALU.mult)\
                        .then_inc(S["sla"], 1)
                if s2:
                    wait(g, S["ov"], c + 1)
                    wait(g, S["ido"], c + 1)
                    wait(g, S[f"d_o{v}"], 8 * (c + 1 - v))
                    hold(g, S["turn_pool"])
                    g.indirect_dma_start(exp_d, bass.IndirectOffsetOnAxis(ap=IDO[:, u, :], axis=0),
                                         OV[:, u, :], None).then_inc(S[f"d_o{u}"], 16)

            phase_a_over(g)
            g.wait_ge(S["tables"], 1)
            g.wait_ge(S["segl"], 1)
            g.wait_ge(S["ef"], 1)
            g.wait_ge(S["states0"], 3)
            turns(g, -1, 4, NCH - 2, NCH, chunk)

            def final(b, u):
                wait(g, S["sq"], 2 * b + 2)
                wait(g, S["rs3"], b)
                hold(g, S["turn_pool"])
                g.tensor_scalar(VE3[:, :], SQ[:, :], 1.0 / D, EPS, ALU.mult, ALU.add).then_inc(S["ve3"], 1)
                wait(g, S["ve3"], b + 1)
                wait(g, S["fo"], 2 * b - 2)
                g.tensor_tensor(RS3[:, u, :], VE3[:, :], mhalf[:, :], ALU.pow).then_inc(S["rs3"], 1)

            turns(g, 0, 4, B - 2, B, final)

        @block.tensor
        def _(pe):
            mm = nc.tensor.matmul
            tr = lambda o, i, n=P: nc.tensor.transpose(o, i, ident[0:n, 0:n])
            pe.wait_ge(S["d_w0"], 16 * 7)
            pe.wait_ge(S["csel"], 1)
            for i, (l, r) in enumerate(((0, 1), (2, 3))):
                for cb in range(KT):
                    for eb in range(KT):
                        last = mm(ps[:, i, cb * D:(cb + 1) * D], wtmp[:, l, eb, cb * P:(cb + 1) * P],
                                  wtmp[:, r, eb, :], start=(eb == 0), stop=(eb == KT - 1))
            for cb in range(KT):
                for eb in range(KT):
                    mm(ps[:, 2, cb:cb + 1], wtmp[:, 0, eb, cb * P:(cb + 1) * P], vtmp[:, 0, eb:eb + 1],
                       start=(eb == 0), stop=(eb == KT - 1))
            for eb in range(KT):
                last = mm(ps[:, 3, 0:D], vtmp[:, 1, eb:eb + 1].broadcast_to([P, P]), wtmp[:, 3, eb, :],
                          start=(eb == 0), stop=(eb == KT - 1))
            last.then_inc(S["m_ps"], 1)
            pe.wait_ge(S["m1"], 1)
            pe.wait_ge(S["m2"], 1)
            pe.wait_ge(S["wb"], 1)
            pe.wait_ge(S["cb"], 1)

            def batch(b, u):
                a1, a2 = within(b, -2, B - 2), within(b, -1, B - 1)
                a3, a4 = within(b, 0, B), within(b, 1, B + 1)
                v = 1 - u
                if a2:
                    m = b + 1
                    wait(pe, S["pT"], m + 1)
                    wait(pe, S["vo"], m + 1)
                    wait(pe, S["x1"], 2 * m)
                    for t in range(TPB):
                        last = mm(ps[:, 2, t * D:(t + 1) * D], PT[:, v, t, :], VO[:, v, :], start=True, stop=True)
                    last.then_inc(S["attn_ps"], 1)
                if a1:
                    m = b + 2
                    wait(pe, S["xn"], m + 1)
                    wait(pe, S["xnT"], m)
                    for t in range(TPB):
                        for k in range(KT):
                            last = tr(ps[:, 0, (t * KT + k) * P:(t * KT + k + 1) * P], XN[:, t, k * P:(k + 1) * P])
                    last.then_inc(S["xnT_ps"], 1)
                    wait(pe, S[f"d_c{u}"], 8 * (m - u) + 16)
                    wait(pe, S["kq"], m)
                    wait(pe, S["vo"], m)
                    for xb in range(KT):
                        for cb in range(KT):
                            mm(ps[:, 6, xb * K:(xb + 1) * K], M1[:, cb, xb * P:(xb + 1) * P], CTX[:, u, cb, :],
                               start=(cb == 0), stop=(cb == KT - 1))
                    for cb in range(KT):
                        mm(ps[:, 6, 2 * K:3 * K], wb[:, cb:cb + 1].broadcast_to([P, P]), CTX[:, u, cb, :],
                           start=(cb == 0), stop=(cb == KT - 1))
                    for cb in range(KT):
                        last = mm(ps[0:K, 6, 256:512], CTX[:, u, cb, :], M2[:, cb, :],
                                  start=(cb == 0), stop=(cb == KT - 1))
                    last.then_inc(S["kq_ps"], 1)
                    wait(pe, S["xnT"], m + 1)
                    wait(pe, S["kq"], m + 1)
                    wait(pe, S["pT"], m)
                    for t in range(TPB):
                        for k in range(KT):
                            last = mm(ps[:, 1, t * K:(t + 1) * K], XNT[:, t, k, :], KQ[:, u, k, :],
                                      start=(k == 0), stop=(k == KT - 1))
                    last.then_inc(S["s_ps"], 1)
                if a3:
                    wait(pe, S["y"], 2 * b + 1)
                    wait(pe, S["yT"], b)
                    for t in range(TPB):
                        for k in range(KT):
                            last = tr(ps[:, 3, (t * KT + k) * P:(t * KT + k + 1) * P],
                                      YB[:, t, k * P:(k + 1) * P])
                    last.then_inc(S["yT_ps"], 1)
                if a4:
                    m = b - 1
                    wait(pe, S["r_mask"], m + 1)
                    wait(pe, S["r_pos"], m)
                    mm(ps[:, 7, 0:TPB * E], triS[:, :], MASK[:, :, :], start=True, stop=True)
                    mm(ps[:, 7, TPB * E:2 * TPB * E], ones[:, :], MASK[:, :, :], start=True, stop=True)\
                        .then_inc(S["rank_ps"], 1)
                if a3:
                    wait(pe, S["yT"], b + 1)
                    wait(pe, S["foldq"], 2)
                    wait(pe, S["rowq"], b)
                    wait(pe, S["r_l2"], b)
                    for t in range(TPB):
                        for k in range(KT):
                            last = mm(ps[:, 4 + t, 0:D + E], YT[:, t, k, :], WQG[:, k, :],
                                      start=(k == 0), stop=(k == KT - 1))
                    last.then_inc(S["qg_ps"], 1)
                if a1:
                    m = b + 2
                    wait(pe, S["p"], m + 1)
                    wait(pe, S["pT"], m)
                    for t in range(TPB):
                        last = tr(ps[0:K, 1, 256 + t * P:256 + (t + 1) * P], PR[:, t, :])
                    last.then_inc(S["pT_ps"], 1)

            turns(pe, -3, 4, B - 4, B + 1, batch)
            pe.wait_ge(S["tables"], 1)
            pe.wait_ge(S["csel"], 4)
            pe.wait_ge(S["cumT"], 1)
            pe.wait_ge(S["foldw"], B)
            pe.wait_ge(S["states0"], 3)
            pe.wait_ge(S["halves"], 4)

            def rows_transposed(m, w):
                wait(pe, S[f"d_row{w}"], 8 * (m - w) + 16)
                wait(pe, S["xT"], m)
                for k in range(4):
                    last = tr(ps[:, 2, k * P:(k + 1) * P], X[:, w, k * P:(k + 1) * P])
                last.then_inc(S["xT_ps"], 1)

            def chunk(c, u):
                n, v = c + 1, 1 - u
                s1, s2 = within(c, -1, NCH - 1), within(c, 0, NCH)
                if s1:
                    e = pe.value_load(ETI[0:1, bass.ds(n, 1)], min_val=0, max_val=E - 1)
                if s1:
                    wait(pe, S["xT"], n + 1)
                    wait(pe, S["kk"], n)
                    mm(ps[:, 0, :], XT[:, v, 0, :], W[:, 0, bass.ds(e * (3 * D), 2 * D)], start=True, stop=False)
                if s2:
                    wait(pe, S["am"], 2 * c + 2)
                    wait(pe, S["qtm"], c + 1)
                    wait(pe, S["hk"], c + 1)
                    for pr in range(2):
                        mm(ps[:, 4, 256 + pr * P:256 + (pr + 1) * P], QTM[:, u, pr, :], HK[:, u, pr, :],
                           start=True, stop=True)
                        for h in (2 * pr, 2 * pr + 1):
                            last = mm(ps[:, 4, 256 + h * HD:256 + (h + 1) * HD], AM[:, u, h, :],
                                      SIN[:, u, h * HD:(h + 1) * HD], start=False, stop=True,
                                      skip_group_check=True)
                    last.then_inc(S["ok_ps"], 1)
                    wait(pe, S["sla"], c + 1)
                    wait(pe, S["hk"], c + 1)
                    wait(pe, S["st"], 2 * c)
                    for h in range(HEADS):
                        q = slice(HD * (h % 2), HD * (h % 2) + HD)
                        last = mm(ps[q, 7, (h // 2) * P:(h // 2 + 1) * P], SLA[:, u, h * HD:(h + 1) * HD],
                                  KV[:, u, :, h, :], start=True, stop=True)
                    last.then_inc(S["h_ps"], 1)
                if s1:
                    wait(pe, S["seg"], n + 1)
                    wait(pe, S["segl"], n)
                    wait(pe, S["rm"], n)
                    wait(pe, S["ef"], n + 1)
                    tr(ps[:, 3, 0:P], META[:, v, 0:1].broadcast_to([P, P])).then_inc(S["seg_ps"], 1)
                    mm(ps[:, 0, :], XT[:, v, 1, :], W[:, 1, bass.ds(e * (3 * D), 2 * D)], start=False, stop=True)\
                        .then_inc(S["fk_ps"], 1)
                if within(c, -1, NCH - 2):
                    rows_transposed(n + 1, u)
                if s2:
                    wait(pe, S["qvg"], c + 1)
                    if s1:
                        wait(pe, S["rm"], n + 1)
                    for pr in range(2):
                        last = tr(ps[:, 3, 256 + pr * P:256 + (pr + 1) * P], QVG[:, pr * P:(pr + 1) * P])
                    last.then_inc(S["qvgT_ps"], 1)
                if s1:
                    wait(pe, S["vv"], n)
                    wait(pe, S["dec"], n)
                    for k in range(KT):
                        last = mm(ps[:, 1, 0:D], XT[:, v, k, :],
                                  W[:, k, bass.ds(e * (3 * D) + 2 * D, D)], start=(k == 0), stop=(k == KT - 1))
                    last.then_inc(S["v_ps"], 1)
                if s2:
                    wait(pe, S["qvgT"], c + 1)
                    wait(pe, S["kT"], 2 * c + 2)
                    for b in range(2):
                        for pr in range(2):
                            last = mm(ps[:, 4 + b, pr * P:(pr + 1) * P], KST[HD * b:HD * b + HD, u, 2 + pr, :],
                                      QVGT[HD * b:HD * b + HD, pr, :], start=True, stop=True)
                        last.then_inc(S["t_ps"], 1)
                if s1:
                    wait(pe, S["ls"], n + 1)
                    wait(pe, S["vv"], n + 1)
                    wait(pe, S["en"], n)
                    wait(pe, S["ef"], n)
                    mm(ps[:, 1, 256:512], cumT[:, :], LS[:, v, 0:D], start=True, stop=True).then_inc(S["g_ps"], 1)
                    for pr in range(2):
                        last = mm(ps[:, 3, 128 + 2 * pr:130 + 2 * pr], LS[:, v, pr * P:(pr + 1) * P], halves[:, :],
                                  start=True, stop=True)
                    last.then_inc(S["f_ps"], 1)
                if s2:
                    wait(pe, S["tm"], 2 * c + 2)
                    wait(pe, S["qvm"], c + 1)
                    wait(pe, S["sp"], c + 1)
                    for pr in range(2):
                        mm(ps[:, 5, 256 + pr * P:256 + (pr + 1) * P], QVM[:, pr, :], SP_[:, u, pr, 1, :, :],
                           start=True, stop=True)
                        for h in (2 * pr, 2 * pr + 1):
                            last = mm(ps[:, 5, 256 + h * HD:256 + (h + 1) * HD], TM[:, h, :], KV[:, u, 1, h, :],
                                      start=False, stop=True, skip_group_check=True)
                    last.then_inc(S["ov_ps"], 1)
                if s1:
                    wait(pe, S["kk"], n + 1)
                    wait(pe, S["sin"], n + 1)
                    wait(pe, S["kT"], 2 * n)
                    for pr in range(2):
                        tr(ps[:, 6, 256 + pr * P:256 + (pr + 1) * P], SIN[:, v, pr * P:(pr + 1) * P])
                    for pr in range(2):
                        last = tr(ps[:, 6, pr * P:(pr + 1) * P], KV[:, v, 0, 2 * pr:2 * pr + 2, :])
                    last.then_inc(S["kT_ps"], 1)
                    wait(pe, S["sp"], n + 1)
                    wait(pe, S["hk"], n)
                    for pr in range(2):
                        last = tr(ps[:, 7, 256 + pr * P:256 + (pr + 1) * P], SP_[:, v, pr, 0, :, :])
                    last.then_inc(S["hk_ps"], 1)
                    wait(pe, S["kT"], 2 * n + 1)
                    wait(pe, S["ov"], c + 1)
                    for b in range(2):
                        for pr in range(2):
                            last = mm(ps[:, 4 + b, pr * P:(pr + 1) * P], KST[HD * b:HD * b + HD, v, pr, :],
                                      XT[HD * b:HD * b + HD, v, 2 + pr, :], start=True, stop=True)
                        last.then_inc(S["a_ps"], 1)

            phase_a_over(pe)
            rows_transposed(0, 0)
            turns(pe, -1, 4, NCH - 2, NCH, chunk)
            pe.wait_ge(S["foldg"], 2)

            def final(b, u):
                if within(b, 0, B):
                    wait(pe, S["os"], b + 1)
                    wait(pe, S["osT"], b)
                    for t in range(TPB):
                        for k in range(KT):
                            last = tr(ps[:, 0, (t * KT + k) * P:(t * KT + k + 1) * P], OS[:, t, k * P:(k + 1) * P])
                    last.then_inc(S["osT_ps"], 1)
                    wait(pe, S["osT"], b + 1)
                    wait(pe, S["fo"], 2 * b - 2)
                    for t in range(TPB):
                        for k in range(KT):
                            last = mm(ps[:, 1 + u, t * D:(t + 1) * D], OT[:, t, k, :], GW[:, k, :],
                                      start=(k == 0), stop=(k == KT - 1))
                    last.then_inc(S["fo_ps"], 1)

            turns(pe, 0, 4, B - 2, B, final)

        @block.scalar
        def _(act):
            A = nc.scalar.activation
            act.preload_act_table_set("natural_log_exp_and_others")
            act.wait_ge(S["m_ps"], 1)
            A(M1[:, :, :], ps[:, 0, :].rearrange("p (k n) -> p k n", k=KT), ACT.Copy).then_inc(S["m1"], 1)
            A(wb[:, :], ps[:, 2, 0:KT], ACT.Copy).then_inc(S["wb"], 1)

            def batch(b, u):
                a1, a3, a4 = within(b, -2, B - 2), within(b, 0, B), within(b, 1, B + 1)
                v = 1 - u
                if isinstance(b, int) and b < 1:
                    q = (b + 3) * E * 3 * D // 4
                    act.dma_start(W[:, :, q:q + E * 3 * D // 4], wfkvT[:, :, q:q + E * 3 * D // 4])\
                        .then_inc(S["d_W"], 16)
                if a4:
                    m = b - 1
                    wait(act, S["lg"], m + 1)
                    wait(act, S["eq"], m)
                    A(AQ[:, :, :], ps[:, 4:6, 0:D], ACT.Abs).then_inc(S["aq"], 1)
                if a1:
                    m = b + 2
                    wait(act, S["rstd1"], 2 * m + 2)
                    wait(act, S["xnT_ps"], m)
                    hold(act, S["turn_act"])
                    for t in range(TPB):
                        last = A(XN[:, t, :], X1[:, bass.ds(m * TPB + t, 1), :].rearrange("p a d -> p (a d)"),
                                 ACT.Identity, bias=MB1[:, u, t:t + 1], scale=RS1[:, u, t:t + 1])
                    last.then_inc(S["xn"], 1)
                if a4:
                    m = b - 1
                    wait(act, S["aq"], m + 1)
                    wait(act, S["lq"], m)
                    A(EQ[:, :, :], AQ[:, :, :], ACT.Exp, scale=-1.0).then_inc(S["eq"], 1)
                    wait(act, S["eq"], m + 1)
                    wait(act, S["rowq"], m)
                    A(LQ[:, :, :], EQ[:, :, :], ACT.Ln, bias=1.0).then_inc(S["lq"], 1)
                if a3:
                    wait(act, S["comb"], 2 * b + 2)
                    wait(act, S["yT_ps"], b)
                    hold(act, S["turn_act"])
                    for t in range(TPB):
                        last = A(YB[:, t, :], X1[:, bass.ds(b * TPB + t, 1), :].rearrange("p a d -> p (a d)"),
                                 ACT.Identity, bias=MB2[:, u, t:t + 1], scale=CO2[:, u, t:t + 1])
                    last.then_inc(S["y"], 1)
                if a1:
                    m = b + 2
                    wait(act, S["xnT_ps"], m + 1)
                    wait(act, S["s_ps"], m)
                    A(XNT[:, :, :, :], ps[:, 0, :].rearrange("p (t k n) -> p t k n", t=TPB, k=KT), ACT.Copy)\
                        .then_inc(S["xnT"], 1)
                if a4:
                    wait(act, S["d_W"], 64)
                    hold(act, S["turn_act"])
                    wp = W[:, v, bass.ds((b - 1 - v) * (WPC // 2), WPC)]
                    A(wp, wp, ACT.Copy, scale=vtmp[:, 2, v:v + 1]).then_inc(S["foldw"], 1)
                if a1:
                    m = b + 2
                    wait(act, S["kq_ps"], m + 1)
                    wait(act, S["s_ps"], m - 1)
                    wait(act, S["ss"], m - 1)
                    A(KQ[:, u], ps[:, 6, 0:3 * K].rearrange("p (a n) -> p a n", a=3), ACT.Copy).then_inc(S["kq"], 1)
                if a4:
                    wait(act, S["lsq"], b)
                    A(EQ[:, :, :], AQ[:, :, :], ACT.Exp).then_inc(S["sgq"], 1)
                if a3:
                    wait(act, S["yT_ps"], b + 1)
                    wait(act, S["qg_ps"], b)
                    A(YT[:, :, :, :], ps[:, 3, :].rearrange("p (t k n) -> p t k n", t=TPB, k=KT), ACT.Copy)\
                        .then_inc(S["yT"], 1)
                if a3:
                    wait(act, S[f"d_scat{u}"], 32 * (b - u))
                    wait(act, S["y"], 2 * b + 1)
                    A(ROW[:, u, :, 0:D], YB[:, :, :], ACT.Copy).then_inc(S["y"], 1)
                if a1:
                    m = b + 2
                    wait(act, S["sm"], m + 1)
                    wait(act, S["pT_ps"], m)
                    wait(act, S["sump"], m)
                    A(PR[:, :, :], SM[:, :, :], ACT.Exp, scale=ISQ).then_inc(S["p"], 1)
                    wait(act, S["pT_ps"], m + 1)
                    wait(act, S["attn_ps"], m - 1)
                    A(PT[:, u], ps[0:K, 1, 256:512].rearrange("p (t n) -> p t n", t=TPB), ACT.Copy)\
                        .then_inc(S["pT"], 1)

            turns(act, -3, 4, B - 4, B + 1, batch)

            def rows_out(m, w):
                wait(act, S["xT_ps"], m + 1)
                wait(act, S["qtm"], m - 1)
                wait(act, S["a_ps"], 2 * m - 2)
                wait(act, S["v_ps"], m - 1)
                A(XT[:, w], ps[:, 2, :].rearrange("p (k n) -> p k n", k=4), ACT.Copy).then_inc(S["xT"], 1)

            def chunk(c, u):
                n, v = c + 1, 1 - u
                s1, s2 = within(c, -1, NCH - 1), within(c, 0, NCH)
                if s2:
                    wait(act, S["sbo"], c + 1)
                    wait(act, S["smo"], c)
                    wait(act, S["qvg"], c)
                    A(EO[:, :], SBO[:, :], ACT.Exp).then_inc(S["eo"], 1)
                if s1:
                    wait(act, S["fk_ps"], n + 1)
                    wait(act, S["ln"], n)
                    A(AB[:, :], ps[:, 0, :], ACT.Abs).then_inc(S["ab"], 1)
                    wait(act, S["ab"], n + 1)
                    A(AB[:, :], AB[:, :], ACT.Exp, scale=-1.0).then_inc(S["ex"], 1)
                    wait(act, S["ex"], n + 1)
                    wait(act, S["ls"], n)
                    A(LN_[:, :], AB[:, :], ACT.Ln, bias=1.0).then_inc(S["ln"], 1)
                    wait(act, S["v_ps"], n + 1)
                    wait(act, S["ov_ps"], n - 1)
                    wait(act, S["h_ps"], n - 1)
                    A(KV[:, v, 1, :, :], ps[:, 1, 0:D].rearrange("p (h d) -> p h d", h=HEADS), ACT.Copy)\
                        .then_inc(S["vv"], 1)
                if within(c, -1, NCH - 2):
                    rows_out(n + 1, u)
                if s1:
                    wait(act, S["ls"], n + 1)
                    wait(act, S["kk"], n)
                    A(SG[:, :], LS[:, v, D:2 * D], ACT.Exp).then_inc(S["sg"], 1)
                    wait(act, S["sin"], n)
                    A(EG[:, :], LS[:, v, 0:D], ACT.Exp, scale=GN).then_inc(S["eg"], 1)
                    wait(act, S["g_ps"], n + 1)
                    A(EN[:, :], ps[:, 1, 256:512], ACT.Exp, scale=-1.0).then_inc(S["en"], 1)
                    wait(act, S["qvg"], n - 1)
                    A(DEC[:, v], ps[:, 1, 256:512], ACT.Exp).then_inc(S["dec"], 1)
                    wait(act, S["f_ps"], n + 1)
                    wait(act, S["fac"], n)
                    A(EF[:, v], ps[:, 3, 128:132].rearrange("p (a b) -> p a b", a=2), ACT.Exp).then_inc(S["ef"], 1)
                    wait(act, S["fac"], n + 1)
                    wait(act, S["st"], 2 * n)
                    wait(act, S["ov_ps"], n - 1)
                    wait(act, S["hk_ps"], n - 1)
                    for pr in range(2):
                        last = A(SP_[:, v, pr], ST[:, pr], ACT.Copy, scale=FAC[:, v, pr:pr + 1])
                    last.then_inc(S["sp"], 1)
                    wait(act, S["kT_ps"], n + 1)
                    wait(act, S["a_ps"], 2 * n - 2)
                    wait(act, S["t_ps"], 2 * n - 2)
                    for a in range(2):
                        A(KST[:, v, 2 * a:2 * a + 2], ps[:, 6, a * 256:a * 256 + 256]
                          .rearrange("p (a n) -> p a n", a=2), ACT.Copy).then_inc(S["kT"], 1)
                    wait(act, S["hk_ps"], n + 1)
                    wait(act, S["ok_ps"], n - 1)
                    A(HK[:, v], ps[:, 7, 256:512].rearrange("p (a n) -> p a n", a=2), ACT.Copy).then_inc(S["hk"], 1)

            phase_a_over(act)
            act.wait_ge(S["states0"], 3)
            rows_out(0, 0)
            turns(act, -1, 4, NCH - 2, NCH, chunk)
            act.wait_ge(S["r_meta"], 2 * B)
            A(RWT[:, :], D21[:, :], ACT.Exp).then_inc(S["rwe"], 1)

            def final(b, u):
                if within(b, 0, B):
                    wait(act, S["os"], b + 1)
                    wait(act, S["ve3"], b)
                    for t in range(TPB):
                        A(SQS[:, :], OS[:, t, :], ACT.Square, accum_out=SQ[:, t:t + 1]).then_inc(S["sq"], 1)
                        wait(act, S["sq"], 2 * b + t + 1)
                    wait(act, S["osT_ps"], b + 1)
                    wait(act, S["fo_ps"], b)
                    A(OT[:, :, :, :], ps[:, 0, :].rearrange("p (t k n) -> p t k n", t=TPB, k=KT), ACT.Copy)\
                        .then_inc(S["osT"], 1)
                if within(b, 1, B + 1):
                    wait(act, S["fo"], 2 * b)
                    act.dma_start(out[bass.ds((b - 1) * T, T), :].rearrange("(t p) d -> p t d", p=P), FO[:, 1 - u])\
                        .then_inc(S[f"d_out{1 - u}"], 16)

            turns(act, 0, 4, B - 2, B + 1, final)
            act.wait_ge(S["d_out0"], 16 * B // 2)
            act.wait_ge(S["d_out1"], 16 * B // 2)

        @block.vector
        def _(dve):
            V = nc.vector
            V.memset(halves[0:64, 0:1], GN).then_inc(S["halves"], 1)
            V.memset(halves[64:128, 0:1], 0.0).then_inc(S["halves"], 1)
            V.memset(halves[0:64, 1:2], 0.0).then_inc(S["halves"], 1)
            V.memset(halves[64:128, 1:2], GN).then_inc(S["halves"], 1)
            dve.wait_ge(S["csel"], 4)
            V.tensor_scalar(cumT[0:64, :], cumT[0:64, :], GN, None, ALU.subtract).then_inc(S["cumT"], 1)
            dve.wait_ge(S["d_w1"], 16 * 4)
            for k in range(KT):
                V.tensor_scalar(WQG[:, k, :], WQG[:, k, :], vtmp[:, 2, k:k + 1], None, ALU.mult)\
                    .then_inc(S["foldq"], 1)
                V.tensor_scalar(GW[:, k, :], GW[:, k, :], gcol[:, k:k + 1], None, ALU.mult).then_inc(S["foldg"], 1)
            dve.wait_ge(S["m_ps"], 1)
            V.tensor_copy(M2[:, :, :], ps[:, 1, :].rearrange("p (k n) -> p k n", k=KT)).then_inc(S["m2"], 1)
            V.tensor_tensor(CBc[:, :], ps[:, 3, 0:D], bob[:, :], ALU.add).then_inc(S["cb"], 1)
            dve.wait_ge(S["iota"], 6)
            V.tensor_copy(BASE[:, 0, 0, :], eoff[:, :]).then_inc(S["r_b2"], 1)
            dve.wait_ge(S["cb"], 1)
            dve.wait_ge(S["r_b2"], 1)

            def bc(ap, n):
                return ap.unsqueeze(2).broadcast_to([P, ap.shape[1], n])

            def batch(b, u):
                a0, a1 = within(b, -3, B - 3), within(b, -2, B - 2)
                a2, a4 = within(b, -1, B - 1), within(b, 1, B + 1)
                v = 1 - u
                lg = LG[:, :, :]
                r = b - 1
                x1_of = lambda m, t: X1[:, bass.ds(m * TPB + t, 1), :].rearrange("p a d -> p (a d)")

                def x1(t):
                    if not a2:
                        return
                    if t == 0:
                        wait(dve, S["attn_ps"], b + 2)
                        wait(dve, S["ri"], b + 2)
                    V.scalar_tensor_tensor(out=x1_of(b + 1, t), in0=ps[:, 2, t * D:(t + 1) * D], scalar=RI[:, t:t + 1],
                                           in1=x1_of(b + 1, t), op0=ALU.mult, op1=ALU.add).then_inc(S["x1"], 1)

                if a4:
                    wait(dve, S["qg_ps"], r + 1)
                    V.tensor_copy(lg, ps[:, 4:6, D:D + E]).then_inc(S["lg"], 1)
                if a0:
                    wait(dve, S[f"d_x{v}"], 8 * (b + 3 - v) + 16)
                    wait(dve, S["stat1"], b + 3)
                    hold(dve, S["turn_dve"])
                    for t in range(TPB):
                        V.bn_stats(BN1[:, t, :], x1_of(b + 3, t)).then_inc(S["bn1"], 1)
                if a4:
                    wait(dve, S["lg"], r + 1)
                    V.tensor_reduce(M1v[:, :], lg, AX, ALU.max).then_inc(S["route"], 1)
                x1(0)
                if a4:
                    wait(dve, S["route"], r * 13 + 1)
                    V.tensor_tensor(EQ1[:, :, :], lg, bc(M1v[:, :], E), ALU.is_equal).then_inc(S["route"], 1)
                x1(1)
                if a4:
                    wait(dve, S["route"], r * 13 + 2)
                    V.tensor_tensor(EQ1[:, :, :], EQ1[:, :, :], wrev[:, :, :], ALU.mult).then_inc(S["route"], 1)
                if a0:
                    wait(dve, S["bn1"], 2 * b + 8)
                    wait(dve, S["rstd1"], 2 * b + 4)
                    hold(dve, S["turn_dve"])
                    for t in range(TPB):
                        last = V.bn_aggr(MV1[:, v, t, :], BN1[:, t, :])
                    last.then_inc(S["stat1"], 1)
                if a4:
                    wait(dve, S["route"], r * 13 + 3)
                    V.tensor_reduce(KEY[:, 0, :], EQ1[:, :, :], AX, ALU.max).then_inc(S["route"], 1)
                if a2:
                    wait(dve, S["x1"], 2 * b + 4)
                    wait(dve, S["stat2"], b + 1)
                    hold(dve, S["turn_dve"])
                    V.bn_stats(BN2[:, 0, :], x1_of(b + 1, 0)).then_inc(S["bn2"], 1)
                if a4:
                    wait(dve, S["route"], r * 13 + 4)
                    V.tensor_tensor(SEL[:, 0], wrev[:, :, :], bc(KEY[:, 0, :], E), ALU.is_equal)\
                        .then_inc(S["route"], 1)
                if a2:
                    V.bn_stats(BN2[:, 1, :], x1_of(b + 1, 1)).then_inc(S["bn2"], 1)
                if a4:
                    wait(dve, S["route"], r * 13 + 5)
                    V.scalar_tensor_tensor(out=L2[:, :, :], in0=SEL[:, 0], scalar=-1e30, in1=lg,
                                           op0=ALU.mult, op1=ALU.add).then_inc(S["r_l2"], 1)
                    wait(dve, S["lq"], r + 1)
                    V.scalar_tensor_tensor(out=AQ[:, :, :], in0=ps[:, 4:6, 0:D], scalar=0.0, in1=LQ[:, :, :],
                                           op0=ALU.min, op1=ALU.subtract).then_inc(S["lsq"], 1)
                    wait(dve, S["r_l2"], r + 1)
                    V.tensor_reduce(M2v[:, :], L2[:, :, :], AX, ALU.max).then_inc(S["route"], 1)
                if a2:
                    wait(dve, S["bn2"], 2 * b + 4)
                    wait(dve, S["comb"], 2 * b)
                    hold(dve, S["turn_dve"])
                    for t in range(TPB):
                        last = V.bn_aggr(MV2[:, v, t, :], BN2[:, t, :])
                    last.then_inc(S["stat2"], 1)
                if a4:
                    wait(dve, S["route"], r * 13 + 6)
                    V.tensor_tensor(EQ1[:, :, :], L2[:, :, :], bc(M2v[:, :], E), ALU.is_equal)\
                        .then_inc(S["route"], 1)
                    V.tensor_tensor(D21[:, bass.ds(r * TPB, TPB)], M2v[:, :], M1v[:, :], ALU.subtract)\
                        .then_inc(S["r_meta"], 1)
                    wait(dve, S["route"], r * 13 + 7)
                    wait(dve, S["y"], 2 * r + 2)
                    V.tensor_tensor(EQ1[:, :, :], EQ1[:, :, :], wrev[:, :, :], ALU.mult).then_inc(S["route"], 1)
                    V.tensor_copy(ROW[:, v, :, CB_], bidx[:, bass.ds(r * TPB, TPB)])
                    V.tensor_copy(ROW[:, v, :, CN_], nidx[:, bass.ds(r * TPB, TPB)])
                    wait(dve, S["route"], r * 13 + 8)
                    V.tensor_reduce(KEY[:, 1, :], EQ1[:, :, :], AX, ALU.max).then_inc(S["route"], 1)
                    V.tensor_scalar(ROW[:, v, :, CE_], KEY[:, 0, :], -1.0, float(E), ALU.mult, ALU.add)\
                        .then_inc(S["r_meta"], 1)
                    wait(dve, S["route"], r * 13 + 9)
                    V.tensor_tensor(SEL[:, 1], wrev[:, :, :], bc(KEY[:, 1, :], E), ALU.is_equal)\
                        .then_inc(S["route"], 1)
                if a1:
                    wait(dve, S["kq"], b + 3)
                    wait(dve, S["attn_ps"], b + 1)
                    V.tensor_tensor(VO[:, u, :], ps[0:K, 6, 256:512], CBc[0:K, :], ALU.add).then_inc(S["vo"], 1)
                if a4:
                    wait(dve, S["route"], r * 13 + 10)
                    V.tensor_tensor(MASK[:, :, :], SEL[:, 0], SEL[:, 1], ALU.add).then_inc(S["r_mask"], 1)
                    wait(dve, S["sgq"], r + 1)
                    V.tensor_tensor(ROW[:, v, :, D:2 * D], ps[:, 4:6, 0:D], EQ[:, :, :], ALU.mult)\
                        .then_inc(S["rowq"], 1)
                if a1:
                    wait(dve, S["s_ps"], b + 3)
                    wait(dve, S["kq"], b + 3)
                    wait(dve, S["sm"], b + 2)
                    V.tensor_tensor(SS[:, :, :], ps[:, 1, 0:TPB * K].rearrange("p (t n) -> p t n", t=TPB),
                                    KQ[:, u, 2, :].unsqueeze(1).broadcast_to([P, TPB, K]), ALU.add)\
                        .then_inc(S["ss"], 1)
                    wait(dve, S["ss"], b + 3)
                    V.tensor_reduce(MX[:, :], SS[:, :, :], AX, ALU.max).then_inc(S["mx"], 1)
                    wait(dve, S["mx"], b + 3)
                    wait(dve, S["p"], b + 2)
                    V.tensor_tensor(SM[:, :, :], SS[:, :, :], bc(MX[:, :], K), ALU.subtract).then_inc(S["sm"], 1)
                if a4:
                    wait(dve, S["rank_ps"], r + 1)
                    V.tensor_tensor(BASE[:, v, 1, :], BASE[:, v, 0, :], ps[:, 7, TPB * E:TPB * E + E], ALU.add)\
                        .then_inc(S["route"], 1)
                    wait(dve, S["route"], r * 13 + 11)
                    V.tensor_tensor(BASE[:, u, 0, :], BASE[:, v, 1, :], ps[:, 7, TPB * E + E:TPB * E + 2 * E],
                                    ALU.add).then_inc(S["r_b2"], 1)
                    V.tensor_tensor(POS[:, :, :], ps[:, 7, 0:TPB * E].rearrange("p (t e) -> p t e", t=TPB),
                                    BASE[:, v], ALU.add).then_inc(S["r_pos"], 1)
                    wait(dve, S["r_b2"], r + 2)
                    wait(dve, S["r_pos"], r + 1)
                    V.tensor_tensor(POSK[:, :, :, :], SEL[:, :, :, :],
                                    POS[:, :, :].unsqueeze(1).broadcast_to([P, 2, TPB, E]), ALU.mult)\
                        .then_inc(S["route"], 1)
                if a1:
                    wait(dve, S["p"], b + 3)
                    V.tensor_reduce(SUM[:, u, :], PR[:, :, :], AX, ALU.add).then_inc(S["sump"], 1)
                if a4:
                    wait(dve, S["route"], r * 13 + 12)
                    V.tensor_reduce(IDF[:, :, :], POSK[:, :, :, :], AX, ALU.add).then_inc(S["route"], 1)
                if a1:
                    wait(dve, S["sump"], b + 3)
                    wait(dve, S["x1"], 2 * b + 4)
                    V.reciprocal(RI[:, :], SUM[:, u, :]).then_inc(S["ri"], 1)
                if a4:
                    wait(dve, S["route"], r * 13 + 13)
                    wait(dve, S[f"d_scat{v}"], 32 * (r - v))
                    V.tensor_copy(IDX[:, v, :], IDF[:, :, :].rearrange("p k t -> p (k t)")).then_inc(S["idx"], 1)

            turns(dve, -3, 4, B - 4, B + 1, batch)

            def step(ins):
                ins.then_inc(S["tab"], 1)
                tab[0] += 1

            def settle():
                dve.wait_ge(S["tab"], tab[0])

            tab = [0]
            dve.wait_ge(S["r_b2"], B + 1)
            dve.wait_ge(S["idx"], B)
            step(V.tensor_tensor(PDF[:, :], BASE[:, 0, 0, :], eoff[:, :], ALU.subtract))
            settle()
            step(V.tensor_scalar(CNTI[:, :], PDF[:, :], float(P - 1), None, ALU.add))
            step(V.tensor_copy(PDI[:, :], BASE[:, 0, 0, :]))
            settle()
            step(V.tensor_scalar(NCI[:, :], CNTI[:, :], 7, None, ALU.arith_shift_right))
            settle()
            step(V.tensor_copy(NCF[:, :], NCI[:, :]))
            settle()
            step(V.tensor_scalar(COEF[:, :], NCF[:, :], float(-P), float(REG), ALU.mult, ALU.add))
            step(V.tensor_copy(CEND[:, 0:1], NCF[:, 0:1]))
            settle()
            for e in range(1, E):
                step(V.tensor_tensor(CEND[:, e:e + 1], CEND[:, e - 1:e], NCF[:, e:e + 1], ALU.add))
                settle()
            step(V.tensor_scalar(RTAB[:, :], cio[:, :], float(P), None, ALU.mult))
            for e in range(E):
                step(V.tensor_scalar(GE[:, e, :], cio[:, :], CEND[:, e:e + 1], None, ALU.is_ge))
            settle()
            step(V.tensor_copy(ECOL[:, :], GE[:, 0, :]))
            settle()
            for e in range(E):
                if e:
                    step(V.tensor_tensor(ECOL[:, :], ECOL[:, :], GE[:, e, :], ALU.add))
                step(V.scalar_tensor_tensor(out=RTAB[:, :], in0=GE[:, e, :], scalar=COEF[:, e:e + 1],
                                            in1=RTAB[:, :], op0=ALU.mult, op1=ALU.add))
                settle()
            step(V.tensor_copy(RTI[:, :], RTAB[:, :]))
            step(V.tensor_scalar(ECOLB[:, :], ECOL[:, :], float(B), None, ALU.mult))
            step(V.tensor_scalar(ETI[:, :], ECOL[:, :], float(E - 1), None, ALU.min))
            settle()
            V.memset(CEND[:, 0:1], 0.0).then_inc(S["tables"], 1)
            phase_a_over(dve)
            V.memset(SP_[:, :, :, :, :, :], 0.0).then_inc(S["states0"], 1)
            V.memset(ST[:, :, :, :, :], 0.0).then_inc(S["states0"], 1)

            dve.wait_ge(S["states0"], 2)
            V.memset(SEGL[:, 1, :], -1.0).then_inc(S["segl"], 1)
            V.memset(EF[:, 1, :, :], 0.0).then_inc(S["ef"], 1)
            V.memset(CONT[:, :, :], 0.0).then_inc(S["states0"], 1)
            dve.wait_ge(S["segl"], 1)
            dve.wait_ge(S["ef"], 1)

            def chunk(c, u):
                n, v = c + 1, 1 - u
                s1, s2 = within(c, -1, NCH - 1), within(c, 0, NCH)
                if s2:
                    wait(dve, S["ok_ps"], c + 1)
                    wait(dve, S["dec"], c + 1)
                    V.tensor_tensor(OKD[:, :], ps[:, 4, 256:512], DEC[:, u], ALU.mult).then_inc(S["okd"], 1)
                    wait(dve, S["okd"], c + 1)
                    V.tensor_reduce(MXO[:, :], OKD[:, :].rearrange("p (h m) -> p h m", h=HEADS), AX, ALU.max)\
                        .then_inc(S["mxo"], 1)
                    wait(dve, S["mxo"], c + 1)
                    wait(dve, S["eo"], c)
                    V.tensor_tensor(SBO[:, :].rearrange("p (h m) -> p h m", h=HEADS),
                                    OKD[:, :].rearrange("p (h m) -> p h m", h=HEADS), bc(MXO[:, :], HD),
                                    ALU.subtract).then_inc(S["sbo"], 1)
                if s1:
                    wait(dve, S["seg_ps"], n + 1)
                    sg = ps[:, 3, 0:P]
                    wait(dve, S["cont"], n)
                    wait(dve, S["sla"], n - 1)
                    V.tensor_copy(SEGL[:, v, :], sg[:, P - 1:P]).then_inc(S["segl"], 1)
                    V.scalar_tensor_tensor(out=MSK[:, v], in0=sg, scalar=META[:, v, 0:1], in1=triM[:, :],
                                           op0=ALU.is_equal, op1=ALU.mult).then_inc(S["msk"], 1)
                    wait(dve, S["qvm"], n - 1)
                    wait(dve, S["qtm"], n - 1)
                    V.tensor_scalar(RM[:, v], sg, SEGL[:, u, :], None, ALU.is_equal).then_inc(S["rm"], 1)
                if s2:
                    wait(dve, S["eo"], c + 1)
                    wait(dve, S["qvgT_ps"], c)
                    V.tensor_tensor(QVG[:, :], EO[:, :], DEC[:, u], ALU.mult).then_inc(S["qvg"], 1)
                    wait(dve, S["qvgT_ps"], c + 1)
                    wait(dve, S["t_ps"], 2 * c)
                    wait(dve, S["qvm"], c)
                    V.tensor_copy(QVGT[:, :, :], ps[:, 3, 256:512].rearrange("p (a n) -> p a n", a=2))\
                        .then_inc(S["qvgT"], 1)
                if s1:
                    wait(dve, S["ln"], n + 1)
                    wait(dve, S["f_ps"], n - 1)
                    wait(dve, S["eg"], n - 1)
                    V.scalar_tensor_tensor(out=LS[:, v, :], in0=ps[:, 0, :], scalar=0.0, in1=LN_[:, :],
                                           op0=ALU.min, op1=ALU.subtract).then_inc(S["ls"], 1)
                if s2:
                    wait(dve, S["msk"], c + 1)
                    wait(dve, S["ov_ps"], c)
                    for b in range(2):
                        wait(dve, S["t_ps"], 2 * c + 1 + b)
                        V.tensor_tensor(TM[:, :, :].rearrange("p (a b) n -> p b a n", b=2)[:, b],
                                        ps[:, 4 + b, 0:256].rearrange("p (a n) -> p a n", a=2),
                                        MSK[:, u].unsqueeze(1).broadcast_to([P, 2, P]), ALU.mult)\
                            .then_inc(S["tm"], 1)
                if s2:
                    wait(dve, S["h_ps"], c + 1)
                    wait(dve, S["sp"], c + 1)
                    wait(dve, S["cont"], c + 1)
                    for h in range(2):
                        q = slice(HD * h, HD * h + HD)
                        V.scalar_tensor_tensor(
                            out=ST[q, :, :, h, :].rearrange("p a k d -> p (a k) d"),
                            in0=SP_[q, u, :, :, h, :].rearrange("p a k d -> p (a k) d"), scalar=CONT[q, u, :],
                            in1=ps[q, 7, 0:256].rearrange("p (a d) -> p a d", a=4),
                            op0=ALU.mult, op1=ALU.add).then_inc(S["st"], 1)
                if s1:
                    wait(dve, S["sg"], n + 1)
                    wait(dve, S["h_ps"], n - 1)
                    V.tensor_tensor(KV[:, v, 0, :, :], ps[:, 0, D:2 * D].rearrange("p (h d) -> p h d", h=HEADS),
                                    SG[:, :].rearrange("p (h d) -> p h d", h=HEADS), ALU.mult).then_inc(S["kk"], 1)
                    wait(dve, S["en"], n + 1)
                    wait(dve, S["eg"], n + 1)
                    wait(dve, S["ok_ps"], n - 1)
                    V.scalar_tensor_tensor(out=SIN[:, v], in0=EG[:, :], scalar=1.0, in1=EN[:, :],
                                           op0=ALU.subtract, op1=ALU.mult, reverse0=True).then_inc(S["sin"], 1)
                if s2:
                    V.tensor_reduce(SMO[:, :], EO[:, :].rearrange("p (h m) -> p h m", h=HEADS), AX, ALU.add)\
                        .then_inc(S["smo"], 1)
                    wait(dve, S["smo"], c + 1)
                    V.reciprocal(RIN[:, u, :], SMO[:, :]).then_inc(S["rin"], 1)
                    wait(dve, S["ov_ps"], c + 1)
                    wait(dve, S["rin"], c + 1)
                    wait(dve, S[f"d_o{u}"], 8 * (c - u))
                    V.tensor_tensor(OV[:, u].rearrange("p (h d) -> p h d", h=HEADS),
                                    ps[:, 5, 256:512].rearrange("p (h d) -> p h d", h=HEADS),
                                    bc(RIN[:, u, :], HD), ALU.mult).then_inc(S["ov"], 1)
                if s1:
                    for b in range(2):
                        wait(dve, S["a_ps"], 2 * n + 1 + b)
                        V.tensor_tensor(AM[:, v].rearrange("p (a b) n -> p b a n", b=2)[:, b],
                                        ps[:, 4 + b, 0:256].rearrange("p (a n) -> p a n", a=2),
                                        MSK[:, v].unsqueeze(1).broadcast_to([P, 2, P]), ALU.mult)\
                            .then_inc(S["am"], 1)

            turns(dve, -1, 4, NCH - 2, NCH, chunk)

            dve.wait_ge(S["rwe"], 1)
            V.tensor_scalar(RW1[:, :], RWT[:, :], 1.0, None, ALU.add).then_inc(S["rwd"], 1)
            dve.wait_ge(S["rwd"], 1)
            V.reciprocal(RW1[:, :], RW1[:, :]).then_inc(S["rw"], 1)
            dve.wait_ge(S["rw"], 1)
            V.tensor_tensor(RW2[:, :], RWT[:, :], RW1[:, :], ALU.mult).then_inc(S["rw"], 1)
            dve.wait_ge(S["rw"], 2)

            def final(b, u):
                v = 1 - u
                if within(b, 0, B):
                    wait(dve, S[f"d_oc{u}"], 16 * (b - u) + 32)
                    wait(dve, S["os"], b)
                    for t in range(TPB):
                        last = V.tensor_scalar(OM[:, t, :], OC[:, u, 1, t, :], RW2[:, bass.ds(b * TPB + t, 1)],
                                               None, ALU.mult)
                    last.then_inc(S["om"], 1)
                    wait(dve, S["om"], b + 1)
                    wait(dve, S["osT_ps"], b)
                    wait(dve, S["sq"], 2 * b)
                    for t in range(TPB):
                        last = V.scalar_tensor_tensor(out=OS[:, t, :], in0=OC[:, u, 0, t, :],
                                                      scalar=RW1[:, bass.ds(b * TPB + t, 1)], in1=OM[:, t, :],
                                                      op0=ALU.mult, op1=ALU.add)
                    last.then_inc(S["os"], 1)
                if within(b, 1, B + 1):
                    wait(dve, S["fo_ps"], b)
                    wait(dve, S["rs3"], b)
                    wait(dve, S[f"d_out{v}"], 8 * (b - 1 - v))
                    for t in range(TPB):
                        V.scalar_tensor_tensor(
                            out=FO[:, v, t, :], in0=ps[:, 1 + v, t * D:(t + 1) * D], scalar=RS3[:, v, t:t + 1],
                            in1=X1[:, bass.ds((b - 1) * TPB + t, 1), :].rearrange("p a d -> p (a d)"),
                            op0=ALU.mult, op1=ALU.add).then_inc(S["fo"], 1)

            turns(dve, 0, 4, B - 2, B + 1, final)


_INS = ['x', 'ctxT', 'wk', 'wq', 'wv', 'woT', 'bqc', 'bvc', 'bo', 'nwc', 'wqgT', 'wfkvT', 'gwc', 'fwoT']


def kernel(x, ctx_1024, L0_xattn_Wk, L0_xattn_Wv, L0_xattn_bv, L0_xattn_Wq, L0_xattn_bq, L0_xattn_Wo, L0_xattn_bo,
           L0_ffn_norm_w, L0_ffn_Wg, L0_ffn_Wq, L0_ffn_Wk, L0_ffn_Wv, L0_ffn_Wf, L0_ffn_gnorm_w, L0_ffn_Wo):
    import numpy as np
    import concourse.bacc as bacc
    from concourse.bass_utils import run_bass_kernel_spmd

    def col(v):
        return np.asarray(v).reshape(KT, P).T

    fkv = np.concatenate([np.asarray(L0_ffn_Wf), np.asarray(L0_ffn_Wk), np.asarray(L0_ffn_Wv)], axis=1)
    fkv = fkv.transpose(2, 0, 1).reshape(KT, P, E * 3 * D).transpose(1, 0, 2)
    data = {
        'x': np.asarray(x).reshape(B * T, D),
        'ctxT': np.asarray(ctx_1024).transpose(0, 2, 1).reshape(B * D, K),
        'wk': L0_xattn_Wk, 'wq': L0_xattn_Wq, 'wv': L0_xattn_Wv, 'woT': np.asarray(L0_xattn_Wo).T,
        'bqc': col(L0_xattn_bq), 'bvc': col(L0_xattn_bv), 'bo': L0_xattn_bo, 'nwc': col(L0_ffn_norm_w),
        'wqgT': np.concatenate([np.asarray(L0_ffn_Wq), np.asarray(L0_ffn_Wg)], axis=0).T,
        'wfkvT': fkv, 'gwc': col(L0_ffn_gnorm_w), 'fwoT': np.asarray(L0_ffn_Wo).T,
    }
    nc = bacc.Bacc("TRN2", target_bir_lowering=False, num_devices=1)
    arrays, args = {}, []
    for name in _INS:
        a = np.ascontiguousarray(data[name])
        arrays[f"in_{name}"] = a
        args.append(nc.dram_tensor(f"in_{name}", a.shape, mybir.dt.from_np(a.dtype), kind="ExternalInput").ap())
    args.append(nc.dram_tensor("out_0", (B * T, D), F32, kind="ExternalOutput").ap())
    xattn_gsa_moe(nc, *args)
    r = run_bass_kernel_spmd(nc, [arrays], core_ids=[0])
    return r.results[0]["out_0"].reshape(B, T, D)
```
